# Optimizing a Trainium2 kernel written in Bass

```python
import numpy as np
import jax
import jax.numpy as jnp

def _softmax(x, axis=-1):
    return jax.nn.softmax(x, axis=axis)

def _gelu(x):
    return jax.nn.gelu(x, approximate=True)

def _silu(x):
    return jax.nn.silu(x)

def _sigmoid(x):
    return jax.nn.sigmoid(x)

def _layernorm(x, axis=-1, eps=1e-05):
    m = jnp.mean(x, axis=axis, keepdims=True)
    v = jnp.var(x, axis=axis, keepdims=True)
    return (x - m) / jnp.sqrt(v + eps)

def _scatter_add(tgt, idx, src, axis=0):
    return tgt.at[idx].add(src)

def _segment_sum(src, seg, n):
    return jax.ops.segment_sum(src, seg, n)
kernel_name = 'mk_decoder_preln_d2_seqx_r2_76016a'

def setup_inputs(seed: int=0):
    np.random.seed(seed)
    _w = jnp.asarray

    def _rec_inputs():
        import jax
        import jax.numpy as jnp
        _rk = jax.random.key(seed)
        x = 7.22e-05 + 1 * jax.random.normal(jax.random.fold_in(_rk, 1), (4, 1024, 512), jnp.float32)
        _lenS = 1024 - jax.random.randint(jax.random.fold_in(_rk, 7), (4,), 0, max(1, 1024 // 4) + 1, jnp.int32)
        _lenS2 = 1024 - jax.random.randint(jax.random.fold_in(_rk, 8), (4,), 0, max(1, 1024 // 4) + 1, jnp.int32)
        _ctx_1024P = jax.random.normal(jax.random.fold_in(_rk, 11), (4, 16, 512), jnp.float32)
        _ctx_1024c = jax.random.dirichlet(jax.random.fold_in(_rk, 511), 0.3 * jnp.ones((16,), jnp.float32), (4, 1024))
        _ctx_1024t = jnp.einsum('bsk,bkd->bsd', _ctx_1024c, _ctx_1024P)
        _ctx_1024t = _ctx_1024t * jax.lax.rsqrt(jnp.mean(jnp.square(_ctx_1024t)) + 1e-12) * 0.953939
        ctx_1024 = 4.13588e-05 + 0.999923 * (_ctx_1024t + 0.3 * jax.random.normal(jax.random.fold_in(_rk, 611), (4, 1024, 512), jnp.float32))
        return (x, ctx_1024)
    x, ctx_1024 = _rec_inputs()

    def _L0_attn_setup():
        import jax, jax.numpy as jnp
        import numpy as np
        HIDDEN = 512
        NUM_HEADS = 16
        HEAD_DIM = HIDDEN // NUM_HEADS
        WINDOW = 33
        PAD = WINDOW // 2
        B, S = (2, 1024)
        key = jax.random.key(seed)
        k = jax.random.split(key, 5)
        x = jax.random.normal(k[0], (B, S, HIDDEN), dtype=jnp.float32)
        w_qkv = jax.random.normal(k[1], (3 * HIDDEN, HIDDEN), dtype=jnp.float32) * 0.02
        b_qkv = jax.random.normal(k[2], (3 * HIDDEN,), dtype=jnp.float32) * 0.02
        w_out = jax.random.normal(k[3], (HIDDEN, HIDDEN), dtype=jnp.float32) * 0.02
        b_out = jax.random.normal(k[4], (HIDDEN,), dtype=jnp.float32) * 0.02
        return {'x': x, 'w_qkv': w_qkv, 'b_qkv': b_qkv, 'w_out': w_out, 'b_out': b_out}
    _L0_attn_all = _L0_attn_setup()
    _L0_attn_in = {k: v for k, v in _L0_attn_all.items() if k in ('w_qkv', 'b_qkv', 'w_out', 'b_out')}
    del _L0_attn_all

    def _L0_xattn_setup():
        import jax, jax.numpy as jnp
        import numpy as np
        WINDOW = 128
        NUM_HEADS = 16

        def _local_attention(q, k, v, w):
            b, h, n, d = q.shape
            nb = n // w
            scale = d ** (-0.5)
            qb = q.reshape(b, h, nb, w, d) * scale
            kb = k.reshape(b, h, nb, w, d)
            vb = v.reshape(b, h, nb, w, d)

            def look_around(x):
                xp = jnp.pad(x, ((0, 0), (0, 0), (1, 0), (0, 0), (0, 0)))
                return jnp.concatenate([xp[:, :, :-1], x], axis=3)
            kw = look_around(kb)
            vw = look_around(vb)
            t = jnp.arange(n).reshape(nb, w)
            tp = jnp.pad(t, ((1, 0), (0, 0)), constant_values=-1)
            kt = jnp.concatenate([tp[:-1], t], axis=1)
            mask = (t[:, :, None] >= kt[:, None, :]) & (kt[:, None, :] >= 0)
            sim = jnp.einsum('bhnwd,bhnjd->bhnwj', qb, kw)
            sim = jnp.where(mask[None, None], sim, -jnp.finfo(sim.dtype).max)
            attn = jax.nn.softmax(sim, axis=-1)
            out = jnp.einsum('bhnwj,bhnjd->bhnwd', attn, vw)
            return out.reshape(b, h, n, d)
        key = jax.random.key(seed)
        k1, k2, k3, k4 = jax.random.split(key, 4)
        B, N, L = (4, 1024, 512)
        return {'query': jax.random.normal(k1, (B, N, L), dtype=jnp.float32), 'key': jax.random.normal(k2, (B, N, L), dtype=jnp.float32), 'value': jax.random.normal(k3, (B, N, L), dtype=jnp.float32), 'W_out': jax.random.normal(k4, (L, L), dtype=jnp.float32) * L ** (-0.5), 'b_out': jnp.zeros((L,), dtype=jnp.float32)}
    _L0_xattn_all = _L0_xattn_setup()
    _L0_xattn_in = {k: v for k, v in _L0_xattn_all.items() if k in ('W_out', 'b_out')}
    del _L0_xattn_all

    def _L0_ffn_setup():
        import jax, jax.numpy as jnp
        import numpy as np
        TOP_K = 2
        key = jax.random.key(seed)
        k1, k2, k3, k4 = jax.random.split(key, 4)
        B_, S, D = (4, 4096, 512)
        E, R = (8, 16)
        x = jax.random.normal(k1, (B_, S, D), dtype=jnp.float32)
        Wg = jax.random.normal(k2, (D, E), dtype=jnp.float32) * 0.02
        A = jax.random.normal(k3, (E, D, R), dtype=jnp.float32) * 0.02
        Bm = jax.random.normal(k4, (E, R, D), dtype=jnp.float32) * 0.02
        return {'x': x, 'Wg': Wg, 'A': A, 'B': Bm}
    _L0_ffn_all = _L0_ffn_setup()
    _L0_ffn_in = {k: v for k, v in _L0_ffn_all.items() if k in ('Wg', 'A', 'B')}
    del _L0_ffn_all

    def _L1_attn_setup():
        import jax, jax.numpy as jnp
        import numpy as np
        B, S, D = (8, 2048, 512)
        WIN = 257
        HALF = WIN // 2
        BL = 128

        def _blockify(t, nb):
            b, s, d = t.shape
            tp = jnp.pad(t, ((0, 0), (BL, BL), (0, 0)))
            tb = tp.reshape(b, nb + 2, BL, d)
            return jnp.concatenate([tb[:, :-2], tb[:, 1:-1], tb[:, 2:]], axis=2)

        def _local_attention(q, k, v):
            b, s, d = q.shape
            nb = s // BL
            qb = q.reshape(b, nb, BL, d)
            kb = _blockify(k, nb)
            vb = _blockify(v, nb)
            scale = 1.0 / np.sqrt(d).astype(np.float32)
            scores = jnp.einsum('bnqd,bnkd->bnqk', qb, kb) * scale
            blk = jnp.arange(nb)[:, None, None]
            r = jnp.arange(BL)[None, :, None]
            c = jnp.arange(3 * BL)[None, None, :]
            i = blk * BL + r
            j = (blk - 1) * BL + c
            rel = j - i
            valid = (rel >= -HALF) & (rel <= HALF) & (j >= 0) & (j < s)
            scores = jnp.where(valid[None], scores, -jnp.inf)
            weights = jax.nn.softmax(scores, axis=-1)
            out = jnp.einsum('bnqk,bnkd->bnqd', weights, vb)
            return out.reshape(b, s, d)
        key = jax.random.key(seed)
        ks = jax.random.split(key, 7)
        s = 0.02
        return {'x': jax.random.normal(ks[0], (B, S, D), jnp.float32), 'Wq': jax.random.normal(ks[1], (D, D), jnp.float32) * s, 'bq': jnp.zeros((D,), jnp.float32), 'Wk': jax.random.normal(ks[2], (D, D), jnp.float32) * s, 'bk': jnp.zeros((D,), jnp.float32), 'Wv': jax.random.normal(ks[3], (D, D), jnp.float32) * s, 'bv': jnp.zeros((D,), jnp.float32)}
    _L1_attn_all = _L1_attn_setup()
    _L1_attn_in = {k: v for k, v in _L1_attn_all.items() if k in ('Wq', 'bq', 'Wk', 'bk', 'Wv', 'bv')}
    del _L1_attn_all

    def _L1_xattn_setup():
        import jax, jax.numpy as jnp
        import numpy as np
        MODEL_DIM = 512
        N_HEADS = 16
        HEAD_DIM = 64
        key = jax.random.key(seed)
        ks = jax.random.split(key, 7)
        B, S = (4, 1024)
        scale = 1.0 / np.sqrt(MODEL_DIM)
        return {'q': jax.random.normal(ks[0], (B, S, MODEL_DIM), dtype=jnp.float32), 'k': jax.random.normal(ks[1], (B, S, MODEL_DIM), dtype=jnp.float32), 'v': jax.random.normal(ks[2], (B, S, MODEL_DIM), dtype=jnp.float32), 'wq': jax.random.normal(ks[3], (N_HEADS * HEAD_DIM, MODEL_DIM), dtype=jnp.float32) * scale, 'wk': jax.random.normal(ks[4], (N_HEADS * HEAD_DIM, MODEL_DIM), dtype=jnp.float32) * scale, 'wv': jax.random.normal(ks[5], (N_HEADS * HEAD_DIM, MODEL_DIM), dtype=jnp.float32) * scale, 'wo': jax.random.normal(ks[6], (MODEL_DIM, N_HEADS * HEAD_DIM), dtype=jnp.float32) * scale}
    _L1_xattn_all = _L1_xattn_setup()
    _L1_xattn_in = {k: v for k, v in _L1_xattn_all.items() if k in ('wq', 'wk', 'wv', 'wo')}
    del _L1_xattn_all

    def _L1_ffn_setup():
        import jax, jax.numpy as jnp
        import numpy as np
        FP8_MAX = 448.0
        FP8 = jnp.float8_e4m3fn
        key = jax.random.key(seed)
        kx, kw, kb = jax.random.split(key, 3)
        B, S, D_in, D_out = (4, 4096, 512, 512)
        x = jax.random.normal(kx, (B, S, D_in), dtype=jnp.float32)
        w = jax.random.normal(kw, (D_out, D_in), dtype=jnp.float32) * 0.02
        weight_scale = jnp.maximum(jnp.max(jnp.abs(w)), 1e-12) / FP8_MAX
        weight = (w / weight_scale).astype(FP8)
        bias = jax.random.normal(kb, (D_out,), dtype=jnp.float32) * 0.01
        return {'x': x, 'weight': weight, 'weight_scale': weight_scale, 'bias': bias}
    _L1_ffn_all = _L1_ffn_setup()
    _L1_ffn_in = {k: v for k, v in _L1_ffn_all.items() if k in ('weight', 'weight_scale', 'bias')}
    del _L1_ffn_all
    return {'x': x, 'ctx_1024': ctx_1024, 'L0_attn_w_qkv': _L0_attn_in['w_qkv'], 'L0_attn_b_qkv': _L0_attn_in['b_qkv'], 'L0_attn_w_out': _L0_attn_in['w_out'], 'L0_attn_b_out': _L0_attn_in['b_out'], 'L0_xattn_W_out': _L0_xattn_in['W_out'], 'L0_xattn_b_out': _L0_xattn_in['b_out'], 'L0_ffn_Wg': _L0_ffn_in['Wg'], 'L0_ffn_A': _L0_ffn_in['A'], 'L0_ffn_B': _L0_ffn_in['B'], 'L1_attn_Wq': _L1_attn_in['Wq'], 'L1_attn_bq': _L1_attn_in['bq'], 'L1_attn_Wk': _L1_attn_in['Wk'], 'L1_attn_bk': _L1_attn_in['bk'], 'L1_attn_Wv': _L1_attn_in['Wv'], 'L1_attn_bv': _L1_attn_in['bv'], 'L1_xattn_wq': _L1_xattn_in['wq'], 'L1_xattn_wk': _L1_xattn_in['wk'], 'L1_xattn_wv': _L1_xattn_in['wv'], 'L1_xattn_wo': _L1_xattn_in['wo'], 'L1_ffn_weight': _L1_ffn_in['weight'], 'L1_ffn_weight_scale': _L1_ffn_in['weight_scale'], 'L1_ffn_bias': _L1_ffn_in['bias']}

def reference(x, ctx_1024, L0_attn_w_qkv, L0_attn_b_qkv, L0_attn_w_out, L0_attn_b_out, L0_xattn_W_out, L0_xattn_b_out, L0_ffn_Wg, L0_ffn_A, L0_ffn_B, L1_attn_Wq, L1_attn_bq, L1_attn_Wk, L1_attn_bk, L1_attn_Wv, L1_attn_bv, L1_xattn_wq, L1_xattn_wk, L1_xattn_wv, L1_xattn_wo, L1_ffn_weight, L1_ffn_weight_scale, L1_ffn_bias):
    import jax
    import jax.numpy as jnp

    def _L0_attn_ref(x, w_qkv, b_qkv, w_out, b_out):
        import jax, jax.numpy as jnp
        import numpy as np
        HIDDEN = 512
        NUM_HEADS = 16
        HEAD_DIM = HIDDEN // NUM_HEADS
        WINDOW = 33
        PAD = WINDOW // 2
        B, S = (2, 1024)
        b, s, _ = x.shape
        qkv = x @ w_qkv.T + b_qkv
        qkv = qkv.reshape(b, s, NUM_HEADS, 3 * HEAD_DIM).transpose(0, 2, 1, 3)
        q, k, v = jnp.split(qkv, 3, axis=-1)
        k_pad = jnp.pad(k, ((0, 0), (0, 0), (PAD, PAD), (0, 0)))
        v_pad = jnp.pad(v, ((0, 0), (0, 0), (PAD, PAD), (0, 0)))
        idx = jnp.arange(s)[:, None] + jnp.arange(WINDOW)[None, :]
        k_win = k_pad[:, :, idx, :]
        v_win = v_pad[:, :, idx, :]
        scores = jnp.einsum('bhsd,bhswd->bhsw', q, k_win) / jnp.sqrt(jnp.asarray(HEAD_DIM, dtype=q.dtype))
        attn = jax.nn.softmax(scores, axis=-1)
        ctx = jnp.einsum('bhsw,bhswd->bhsd', attn, v_win)
        ctx = ctx.transpose(0, 2, 1, 3).reshape(b, s, HIDDEN)
        return ctx @ w_out.T + b_out

    def _L0_xattn_ref(query, key, value, W_out, b_out):
        import jax, jax.numpy as jnp
        import numpy as np
        WINDOW = 128
        NUM_HEADS = 16

        def _local_attention(q, k, v, w):
            b, h, n, d = q.shape
            nb = n // w
            scale = d ** (-0.5)
            qb = q.reshape(b, h, nb, w, d) * scale
            kb = k.reshape(b, h, nb, w, d)
            vb = v.reshape(b, h, nb, w, d)

            def look_around(x):
                xp = jnp.pad(x, ((0, 0), (0, 0), (1, 0), (0, 0), (0, 0)))
                return jnp.concatenate([xp[:, :, :-1], x], axis=3)
            kw = look_around(kb)
            vw = look_around(vb)
            t = jnp.arange(n).reshape(nb, w)
            tp = jnp.pad(t, ((1, 0), (0, 0)), constant_values=-1)
            kt = jnp.concatenate([tp[:-1], t], axis=1)
            mask = (t[:, :, None] >= kt[:, None, :]) & (kt[:, None, :] >= 0)
            sim = jnp.einsum('bhnwd,bhnjd->bhnwj', qb, kw)
            sim = jnp.where(mask[None, None], sim, -jnp.finfo(sim.dtype).max)
            attn = jax.nn.softmax(sim, axis=-1)
            out = jnp.einsum('bhnwj,bhnjd->bhnwd', attn, vw)
            return out.reshape(b, h, n, d)
        b, n, latent = query.shape
        h = NUM_HEADS
        d = latent // h
        q = query.reshape(b, n, h, d).transpose(0, 2, 1, 3)
        k = key.reshape(b, n, h, d).transpose(0, 2, 1, 3)
        v = value.reshape(b, n, h, d).transpose(0, 2, 1, 3)
        x = _local_attention(q, k, v, WINDOW)
        x = x.transpose(0, 2, 1, 3).reshape(b, n, h * d)
        return x @ W_out.T + b_out

    def _L0_ffn_ref(x, Wg, A, B):
        import jax, jax.numpy as jnp
        import numpy as np
        TOP_K = 2
        D = x.shape[-1]
        E = Wg.shape[-1]
        xs = x.reshape(-1, D)
        gate_logits = xs @ Wg
        topw, sel = jax.lax.top_k(gate_logits, TOP_K)
        topw = jax.nn.softmax(topw.astype(jnp.float32), axis=-1).astype(x.dtype)
        cw = jnp.sum(jax.nn.one_hot(sel, E, dtype=x.dtype) * topw[..., None], axis=1)
        h = jnp.einsum('td,edr->ter', xs, A)
        hw = h * cw[..., None]
        out = jnp.einsum('ter,erd->td', hw, B)
        return out.reshape(x.shape)

    def _L1_attn_ref(x, Wq, bq, Wk, bk, Wv, bv):
        import jax, jax.numpy as jnp
        import numpy as np
        B, S, D = (8, 2048, 512)
        WIN = 257
        HALF = WIN // 2
        BL = 128

        def _blockify(t, nb):
            b, s, d = t.shape
            tp = jnp.pad(t, ((0, 0), (BL, BL), (0, 0)))
            tb = tp.reshape(b, nb + 2, BL, d)
            return jnp.concatenate([tb[:, :-2], tb[:, 1:-1], tb[:, 2:]], axis=2)

        def _local_attention(q, k, v):
            b, s, d = q.shape
            nb = s // BL
            qb = q.reshape(b, nb, BL, d)
            kb = _blockify(k, nb)
            vb = _blockify(v, nb)
            scale = 1.0 / np.sqrt(d).astype(np.float32)
            scores = jnp.einsum('bnqd,bnkd->bnqk', qb, kb) * scale
            blk = jnp.arange(nb)[:, None, None]
            r = jnp.arange(BL)[None, :, None]
            c = jnp.arange(3 * BL)[None, None, :]
            i = blk * BL + r
            j = (blk - 1) * BL + c
            rel = j - i
            valid = (rel >= -HALF) & (rel <= HALF) & (j >= 0) & (j < s)
            scores = jnp.where(valid[None], scores, -jnp.inf)
            weights = jax.nn.softmax(scores, axis=-1)
            out = jnp.einsum('bnqk,bnkd->bnqd', weights, vb)
            return out.reshape(b, s, d)
        q = x @ Wq + bq
        k = x @ Wk + bk
        v = x @ Wv + bv
        return _local_attention(q, k, v)

    def _L1_xattn_ref(q, k, v, wq, wk, wv, wo):
        import jax, jax.numpy as jnp
        import numpy as np
        MODEL_DIM = 512
        N_HEADS = 16
        HEAD_DIM = 64
        B, Sq, _ = q.shape
        Sk = k.shape[1]
        qh = (q @ wq.T).reshape(B, Sq, N_HEADS, HEAD_DIM).transpose(0, 2, 1, 3)
        kh = (k @ wk.T).reshape(B, Sk, N_HEADS, HEAD_DIM).transpose(0, 2, 1, 3)
        vh = (v @ wv.T).reshape(B, Sk, N_HEADS, HEAD_DIM).transpose(0, 2, 1, 3)
        scores = jnp.einsum('bhqd,bhkd->bhqk', qh, kh) / jnp.sqrt(jnp.float32(HEAD_DIM))
        attn = jax.nn.softmax(scores, axis=-1)
        ctx = jnp.einsum('bhqk,bhkd->bhqd', attn, vh)
        ctx = ctx.transpose(0, 2, 1, 3).reshape(B, Sq, N_HEADS * HEAD_DIM)
        return ctx @ wo.T

    def _L1_ffn_ref(x, weight, weight_scale, bias):
        import jax, jax.numpy as jnp
        import numpy as np
        FP8_MAX = 448.0
        FP8 = jnp.float8_e4m3fn
        amax = jnp.max(jnp.abs(x), axis=-1, keepdims=True)
        x_scale = jnp.maximum(amax, 1e-12) / FP8_MAX
        qinput = (x / x_scale).astype(FP8)
        A = qinput.astype(x.dtype) * x_scale
        Bm = weight.astype(x.dtype) * weight_scale
        out = jnp.einsum('bsk,nk->bsn', A, Bm) + bias
        return out.astype(x.dtype)
    x = x + _L0_attn_ref(_layernorm(x, axis=-1), L0_attn_w_qkv, L0_attn_b_qkv, L0_attn_w_out, L0_attn_b_out)
    x = x + _L0_xattn_ref(_layernorm(x, axis=-1), ctx_1024, ctx_1024, L0_xattn_W_out, L0_xattn_b_out)
    x = x + _L0_ffn_ref(_layernorm(x, axis=-1), L0_ffn_Wg, L0_ffn_A, L0_ffn_B)
    x = x + _L1_attn_ref(_layernorm(x, axis=-1), L1_attn_Wq, L1_attn_bq, L1_attn_Wk, L1_attn_bk, L1_attn_Wv, L1_attn_bv)
    x = x + _L1_xattn_ref(_layernorm(x, axis=-1), ctx_1024, ctx_1024, L1_xattn_wq, L1_xattn_wk, L1_xattn_wv, L1_xattn_wo)
    x = x + _L1_ffn_ref(_layernorm(x, axis=-1), L1_ffn_weight, L1_ffn_weight_scale, L1_ffn_bias)
    return x

_drawn_inputs = setup_inputs


def setup_inputs(seed=0):
    import zlib

    import numpy as np

    out = dict(_drawn_inputs(seed))
    spreads = {'L0_xattn_b_out': (0.0, 0.1),
     'L1_attn_bq': (0.0, 0.8),
     'L1_attn_bk': (0.0, 0.8),
     'L1_attn_bv': (0.0, 0.1)}
    factors = {'L0_attn_b_qkv': 5.979,
     'L0_attn_b_out': 3.164,
     'L0_ffn_Wg': 3.229,
     'L0_ffn_A': 2.773,
     'L0_ffn_B': 2.832,
     'L1_attn_Wq': 8.0,
     'L1_attn_Wk': 8.0,
     'L1_ffn_bias': 8.0}
    for name, (base, spread) in spreads.items():
        noise = np.random.default_rng([zlib.crc32(name.encode()), seed]).standard_normal(out[name].shape)
        drawn = base * np.exp(spread * noise) if base else spread * noise
        out[name] = jnp.asarray(drawn.astype(out[name].dtype))
    for name, factor in factors.items():
        out[name] = (out[name] * factor).astype(out[name].dtype)
    return out
```

```python
from contextlib import ExitStack

import concourse.bass as bass
from concourse import mybir

F32 = mybir.dt.float32
F16 = mybir.dt.float16
BF16 = mybir.dt.bfloat16
U8 = mybir.dt.uint8
U16 = mybir.dt.uint16
U32 = mybir.dt.uint32
F8 = mybir.dt.float8e4
ALU = mybir.AluOpType
ACT = mybir.ActivationFunctionType
X_AXIS = mybir.AxisListType.X

B = 4
S = 1024
D = 512
P = 128
NT = S // P
KC = D // P
EPS = 1e-5
WS = 64.0
BIAS_LO = 32
BIAS_P = BIAS_LO + 1
MASKED = -1e30

TERMS = ((0, 0), (0, 1), (1, 0))


def tokens_in(ap, b, t):
    return ap[bass.ds(b * S + t * P, P), :]


def scoped(nc):
    stack, sems = ExitStack(), []

    def clear():
        if sems:
            nc.clear_and_free_semaphores(sems)
            nc.all_engine_barrier()

    def sem(name):
        sems.append(nc.alloc_semaphore(name=name))
        return sems[-1]

    stack.callback(clear)
    sb = lambda name, shape, dt: stack.enter_context(nc.sbuf_tensor(name, shape, dt))
    return stack, sb, sem


class Constants:

    def __init__(self, sb, sem):
        self.ident, self.ident_b = sb("ident", [P, P], F32), sb("ident_b", [P, P], BF16)
        self.ones = sb("ones", [BIAS_P, S], F16)
        self.minus_half, self.eps = sb("minus_half", [P, NT], F32), sb("eps", [P, NT], F32)
        self.x_loaded = [sem(f"x_loaded{t}") for t in range(NT)]
        self.stored = [sem(f"stored{t}") for t in range(NT)]
        self.turn = 0


def constants(nc, sb, sem):
    c = Constants(sb, sem)
    filled = sem("const_filled")
    with nc.Block() as block:
        @block.gpsimd
        def _(pool):
            pool.memset(c.ident[:, :], 0.0).then_inc(filled, 1)
            pool.memset(c.ident_b[:, :], 0.0).then_inc(filled, 1)
            pool.memset(c.ones[:, :], 1.0).then_inc(filled, 1)
            pool.memset(c.minus_half[:, :], -0.5).then_inc(filled, 1)
            pool.memset(c.eps[:, :], EPS).then_inc(filled, 1)
            pool.wait_ge(filled, 5)
            for m in (c.ident, c.ident_b):
                pool.affine_select(out=m[:, :], in_=m[:, :], compare_op=ALU.not_equal, fill=1.0, base=0,
                                   pattern=[[-1, P]], channel_multiplier=1).then_inc(filled, 1)
            pool.wait_ge(filled, 7)
    return c


def split_weights(nc, tag, jobs, biases=()):
    stack, sb, sem = scoped(nc)
    with stack:
        stage = sb(f"{tag}_stage", [P, 4, 2048], F32)
        bias_stage = sb(f"{tag}_bias_stage", [BIAS_P, max(1, len(biases)), D], F32)
        loaded = [sem(f"{tag}_w_loaded{i}") for i in range(4)]
        bias_zeroed, bias_loaded = sem(f"{tag}_bias_zeroed"), sem(f"{tag}_bias_loaded")
        hi_ready, lo_ready, bias_hi = sem(f"{tag}_w_hi"), sem(f"{tag}_w_lo"), sem(f"{tag}_bias_hi")

        def staged(i):
            k, n = jobs[i][0].shape[1:]
            return stage[:, i % 4, 0:k * n].rearrange("p (k n) -> p k n", n=n)

        with nc.Block() as block:
            @block.sync
            def _(sp):
                for i, (_, _, dram) in enumerate(jobs):
                    if i >= 4:
                        sp.wait_ge(lo_ready, i - 3)
                    sp.dma_start(staged(i), dram).then_inc(loaded[i % 4], 16)
                if biases:
                    sp.wait_ge(bias_zeroed, 1)
                    for i, (_, dram) in enumerate(biases):
                        for p in (0, BIAS_LO):
                            sp.dma_start(bias_stage[p:p + 1, i, :], dram).then_inc(bias_loaded, 16)

            @block.scalar
            def _(act):
                for i, (hi, _, _) in enumerate(jobs):
                    act.wait_ge(loaded[i % 4], 16 * (i // 4 + 1))
                    act.activation(hi, staged(i), ACT.Copy, scale=WS).then_inc(hi_ready, 1)
                if biases:
                    act.wait_ge(bias_loaded, 32 * len(biases))
                    for i, (rows, _) in enumerate(biases):
                        act.activation(rows, bias_stage[:, i, :], ACT.Copy, scale=WS).then_inc(bias_hi, 1)

            @block.vector
            def _(dve):
                if biases:
                    dve.memset(bias_stage[:, :, :], 0.0).then_inc(bias_zeroed, 1)
                for i, (hi, lo, _) in enumerate(jobs):
                    dve.wait_ge(hi_ready, i + 1)
                    dve.scalar_tensor_tensor(out=lo, in0=staged(i), scalar=WS, in1=hi,
                                             op0=ALU.mult, op1=ALU.subtract).then_inc(lo_ready, 1)
                for i, (rows, _) in enumerate(biases):
                    dve.wait_ge(bias_hi, i + 1)
                    low = rows[BIAS_LO:BIAS_P, :]
                    dve.scalar_tensor_tensor(out=low, in0=bias_stage[BIAS_LO:BIAS_P, i, :], scalar=WS, in1=low,
                                             op0=ALU.mult, op1=ALU.subtract).then_inc(lo_ready, 1)
                dve.wait_ge(lo_ready, len(jobs) + len(biases))


def square_jobs(pair, dram, cols=D):
    view = dram.rearrange("(k p) n -> p k n", p=P)
    step = max(1, 2048 // cols)
    kc = view.shape[1]
    return [(pair[0][:, k:k + step, :], pair[1][:, k:k + step, :], view[:, k:k + step, :])
            for k in range(0, kc, step)]



NORM_BANKS = (6, 7)


class Norm:

    def __init__(self, nc, sb, sem, tag, consts, psum, width=S, first=0, scale=1.0):
        self.x = sb(f"{tag}_x", [P, NT, D], F32)
        self.stats, self.mv = sb(f"{tag}_stats", [P, NT, 6], F32), sb(f"{tag}_mv", [P, NT, 2], F32)
        self.rstd, self.fence = sb(f"{tag}_rstd", [P, NT], F32), sb(f"{tag}_fence", [P, 1], F32)
        self.xn = sb(f"{tag}_xn", [P, 2, D], F32)
        self.xt = [sb(f"{tag}_xt{p}", [P, KC, width], F16) for p in range(2)]
        self.first, self.scale, self.consts, self.psum = first, scale, consts, psum
        self.x_loaded, self.stored, self.turn = consts.x_loaded, consts.stored, consts.turn * B
        self.moments, self.eps_added = sem(f"{tag}_moments"), sem(f"{tag}_eps_added")
        self.rstd_ready, self.xn_ready = sem(f"{tag}_rstd_ready"), sem(f"{tag}_xn_ready")
        self.xn_transposed = sem(f"{tag}_xn_transposed")
        self.xt_hi, self.xt_lo = sem(f"{tag}_xt_hi"), sem(f"{tag}_xt_lo")
        self.res_ready = sem(f"{tag}_res_ready")


def norm_gpsimd(pool, n, b):
    pool.wait_ge(n.moments, 2 * NT * (b + 1))
    pool.tensor_tensor(n.rstd[:, :], n.mv[:, :, 1], n.consts.eps[:, :], ALU.add).then_inc(n.eps_added, 1)
    pool.wait_ge(n.eps_added, b + 1)
    pool.tensor_tensor(n.rstd[:, :], n.rstd[:, :], n.consts.minus_half[:, :], ALU.pow).then_inc(n.rstd_ready, 1)


def norm_moments(dve, n, b):
    for t in range(NT):
        dve.wait_ge(n.x_loaded[t], 16 * b + 16 * (n.turn + 1))
        dve.bn_stats(n.stats[:, t, :], n.x[:, t, :]).then_inc(n.moments, 1)
    dve.wait_ge(n.moments, 2 * NT * b + NT)
    dve.memset(n.fence[:, :], 0.0)
    for t in range(NT):
        dve.bn_aggr(n.mv[:, t, :], n.stats[:, t, :]).then_inc(n.moments, 1)
    dve.wait_ge(n.rstd_ready, b + 1)


def norm_vector(dve, n, b):
    norm_moments(dve, n, b)

    def normalize(t):
        if t >= 2:
            dve.wait_ge(n.xn_transposed, NT * b + t - 1)
        dve.tensor_scalar(n.xn[:, t % 2, :], n.x[:, t, :], n.mv[:, t, 0:1], n.rstd[:, t:t + 1],
                          ALU.subtract, ALU.mult).then_inc(n.xn_ready, 1)

    normalize(0)
    for t in range(NT):
        if t + 1 < NT:
            normalize(t + 1)
        bank = n.psum[:, NORM_BANKS[t % 2], :].rearrange("p (k c) -> p k c", c=P)
        cols = slice(n.first + t * P, n.first + (t + 1) * P)
        dve.wait_ge(n.xt_hi, NT * b + t + 1)
        dve.scalar_tensor_tensor(out=n.xt[1][:, :, cols], in0=bank, scalar=n.scale, in1=n.xt[0][:, :, cols],
                                 op0=ALU.mult, op1=ALU.subtract).then_inc(n.xt_lo, 1)


def norm_tensor(pe, n, b):
    for t in range(NT):
        pe.wait_ge(n.xn_ready, NT * b + t + 1)
        if t >= 2:
            pe.wait_ge(n.xt_lo, NT * b + t - 1)
        for k in range(KC):
            last = pe.transpose(n.psum[:, NORM_BANKS[t % 2], k * P:(k + 1) * P],
                                n.xn[:, t % 2, k * P:(k + 1) * P], n.consts.ident[:, :])
        last.then_inc(n.xn_transposed, 1)


def norm_scalar(act, n, b):
    for t in range(NT):
        bank = n.psum[:, NORM_BANKS[t % 2], :].rearrange("p (k c) -> p k c", c=P)
        cols = slice(n.first + t * P, n.first + (t + 1) * P)
        act.wait_ge(n.xn_transposed, NT * b + t + 1)
        act.activation(n.xt[0][:, :, cols], bank, ACT.Copy, scale=n.scale).then_inc(n.xt_hi, 1)


def stream_rows(sp, n, x_in, x_out, between=None):
    def load(b, t):
        sp.dma_start(n.x[:, t, :], tokens_in(x_in, b, t)).then_inc(n.x_loaded[t], 16)

    def store(b, t):
        sp.wait_ge(n.res_ready, NT * b + t + 1)
        sp.dma_start(tokens_in(x_out, b, t), n.x[:, t, :]).then_inc(n.stored[t], 16)

    for t in range(NT):
        load(0, t)
    with sp.Fori(0, B - 1) as b:
        if between is not None:
            between(b)
        for t in range(NT + 1):
            if t < NT:
                store(b, t)
            if t >= 1:
                sp.wait_ge(n.stored[t - 1], 16 * b + 16 * (n.turn + 1))
                load(b + 1, t - 1)
    for t in range(NT):
        store(B - 1, t)
    for t in range(NT):
        sp.wait_ge(n.stored[t], 16 * (n.turn + B))


class OutProjection:

    def __init__(self, ot, wo, bias, projected):
        self.ot, self.wo, self.bias, self.projected = ot, wo, bias, projected


def out_projection_tensor(pe, n, o, b):
    chunks = o.wo[0].shape[1]
    for t in range(NT):
        if t >= 4:
            pe.wait_ge(n.res_ready, NT * b + t - 3)
        for i, (k, (p, q)) in enumerate((k, term) for k in range(chunks) for term in TERMS):
            last = pe.matmul(n.psum[:, t % 4, :], o.ot[p][:, k, t * P:(t + 1) * P], o.wo[q][:, k, :],
                             start=(i == 0), stop=(i == 3 * chunks - 1 and o.bias is None))
        if o.bias is not None:
            last = pe.matmul(n.psum[:, t % 4, :], n.consts.ones[:, 0:P], o.bias, start=False, stop=True)
        last.then_inc(o.projected, 1)


def out_projection_vector(dve, n, o, b):
    for t in range(NT):
        dve.wait_ge(o.projected, NT * b + t + 1)
        dve.scalar_tensor_tensor(out=n.x[:, t, :], in0=n.psum[:, t % 4, :], scalar=1 / WS, in1=n.x[:, t, :],
                                 op0=ALU.mult, op1=ALU.add).then_inc(n.res_ready, 1)



H = 16
DH = D // H
GR = P // DH
VC = DH + 1
FLIP_BANKS = (4, 5)


class LocalHeads:

    def __init__(self, nc, sb, sem, tag, consts, psum, tiles, rows, blocks, mask, qt, kt, v, ot):
        self.consts, self.psum, self.mask = consts, psum, mask
        self.qt, self.kt, self.v, self.ot = qt, kt, v, ot
        self.tiles, self.rows, self.blocks = tiles, rows, blocks
        self.chunks = 4 // blocks
        self.heads = 2 * self.chunks
        self.per_tile = H // self.heads
        self.units = tiles * self.per_tile
        self.probs = sb(f"{tag}_probs", [P, 2, 2, self.chunks, blocks * P], F32)
        self.pt = [sb(f"{tag}_pt{p}", [P, 2, 2, 4, P], F16) for p in range(2)]
        self.neg_max = sb(f"{tag}_neg_max", [P, 2, self.heads], F32)
        self.inv_sum = sb(f"{tag}_inv_sum", [P, 2, self.heads], F32)
        self.out = sb(f"{tag}_heads_out", [P, 2, KC, 2, 2, DH], F32)
        self.scored, self.maxed, self.exped = (sem(f"{tag}_{s}") for s in ("scored", "maxed", "exped"))
        self.flipped, self.flip_hi, self.flip_lo = (sem(f"{tag}_{s}") for s in ("flipped", "flip_hi", "flip_lo"))
        self.weighted, self.summed, self.normed = (sem(f"{tag}_{s}") for s in ("weighted", "summed", "normed"))
        self.order = [g for step in range(self.units + 2) for g in self.groups(step)]
        self.place = {g: i for i, g in enumerate(self.order)}

    def unit(self, u):
        tile, at = divmod(u, self.per_tile)
        return tile, (at // 2) * self.chunks, at % 2

    def first_key(self, u):
        return P if self.blocks == 2 and u < self.per_tile else 0

    def unit_groups(self, u):
        return [("probs", u, i) for i in range(2) if not (self.first_key(u) and i == 0)]

    def groups(self, step):
        mine = self.unit_groups(step) if step < self.units else []
        done = step - 2
        out = [("out", done // self.per_tile, 0)] if done >= 0 and done % self.per_tile == self.per_tile - 1 else []
        return mine + out

    def first_exps(self, u, i):
        return self.heads if self.blocks == 2 else 4 * (i + 1)

    def bank(self, group):
        f = self.place[group]
        return self.psum[:, FLIP_BANKS[f % 2], :].rearrange("p (h q) -> p h q", q=P)[:, :, 0:self.rows]

    def destination(self, group):
        kind, index, i = group
        if kind == "probs":
            return [self.pt[p][:, index % 2, i, :, 0:self.rows] for p in range(2)]
        return [self.ot[p][:, :, index * self.rows:(index + 1) * self.rows] for p in range(2)]

    def scores(self, u):
        return self.psum[:, 2 * (u % 2):2 * (u % 2) + 2, :]\
            .rearrange("p j (g c) -> p (j g) c", c=self.blocks * P)[:, :, self.first_key(u):]


    def score(self, pe, u):
        tile, g0, s = self.unit(u)
        k0, width = self.first_key(u), self.blocks * P
        queries = slice(tile * self.rows, tile * self.rows + P)
        first = (tile - 1) * P + k0 if self.blocks == 2 else tile * self.rows
        keys = slice(first, first + width - k0)
        for g in range(self.chunks):
            for i, (p, q) in enumerate(TERMS):
                for j in range(2):
                    r = slice(DH * (2 * s + j), DH * (2 * s + j + 1))
                    last = pe.matmul(self.psum[:, 2 * (u % 2) + j, g * width + k0:(g + 1) * width],
                                     self.qt[p][r, g0 + g, queries], self.kt[q][r, g0 + g, keys],
                                     start=(i == 0), stop=(i == 2))
                if i == 0:
                    for j in range(2):
                        pe.matmul(self.psum[:, 2 * (u % 2) + j, (g + 1) * width - P:(g + 1) * width],
                                  self.consts.ident_b[:, :], self.mask[:, :], start=False, stop=False)
        last.then_inc(self.scored, 1)

    def flip(self, pe, b, group):
        kind, index, i = group
        f = self.place[group]
        bank = self.psum[:, FLIP_BANKS[f % 2], :]
        if f >= 2:
            pe.wait_ge(self.flip_lo, len(self.order) * b + f - 1)
        if kind == "probs":
            pe.wait_ge(self.exped, self.heads * (self.units * b + index) + self.first_exps(index, i))
            for slot in range(4):
                g, j = slot // 2, slot % 2
                if self.blocks == 2:
                    source = self.probs[:, index % 2, j, g, i * P:(i + 1) * P]
                else:
                    source = self.probs[:, index % 2, j, 2 * i + g, :]
                last = pe.transpose(bank[:, slot * P:(slot + 1) * P], source, self.consts.ident[:, :])
        else:
            pe.wait_ge(self.normed, self.units * b + (index + 1) * self.per_tile)
            for k in range(KC):
                last = pe.transpose(bank[:, k * P:(k + 1) * P],
                                    self.out[:, index % 2, k, :, :, :].rearrange("p a j d -> p (a j d)"),
                                    self.consts.ident[:, :])
        last.then_inc(self.flipped, 1)

    def weigh(self, pe, b, u):
        tile, g0, s = self.unit(u)
        for group in self.unit_groups(u):
            pe.wait_ge(self.flip_lo, len(self.order) * b + self.place[group] + 1)
        if u >= 2:
            pe.wait_ge(self.normed, self.units * b + u - 1)
        for g in range(self.chunks):
            for j in range(2):
                head, at = GR * (g0 + g) + 2 * s + j, g * 2 + j
                if self.blocks == 2:
                    parts = [(i, at, tile - 1 + i) for i in range(self.first_key(u) // P, 2)]
                else:
                    parts = [(at // 4, at % 4, tile)]
                terms = [(*part, p, q) for part in parts for p, q in TERMS]
                for n, (i, slot, block, p, q) in enumerate(terms):
                    last = pe.matmul(self.psum[:, 6 + u % 2, at * VC:(at + 1) * VC],
                                     self.pt[p][:, u % 2, i, slot, :], self.v[q][:, block, head, :],
                                     start=(n == 0), stop=(n == len(terms) - 1))
        last.then_inc(self.weighted, 1)

    def tensor(self, pe, b):
        self.score(pe, 0)
        for step in range(self.units + 2):
            if step + 1 < self.units:
                self.score(pe, step + 1)
            for group in self.groups(step):
                self.flip(pe, b, group)
            if 1 <= step <= self.units:
                self.weigh(pe, b, step - 1)
        pe.wait_ge(self.flip_lo, len(self.order) * (b + 1))


    def exponentials(self, act, b, u):
        act.wait_ge(self.maxed, self.units * b + u + 1)
        k0, width = self.first_key(u), self.blocks * P
        for g in range(self.chunks):
            for j in range(2):
                h = self.chunks * j + g
                act.activation(self.probs[:, u % 2, j, g, k0:],
                               self.psum[:, 2 * (u % 2) + j, g * width + k0:(g + 1) * width], ACT.Exp,
                               bias=self.neg_max[:, u % 2, h:h + 1]).then_inc(self.exped, 1)

    def scalar(self, act, b):
        self.exponentials(act, b, 0)
        for step in range(self.units + 2):
            for group in self.groups(step):
                act.wait_ge(self.flipped, len(self.order) * b + self.place[group] + 1)
                act.activation(self.destination(group)[0], self.bank(group), ACT.Copy).then_inc(self.flip_hi, 1)
            if step + 1 < self.units:
                self.exponentials(act, b, step + 1)


    def maxima(self, dve, b, u):
        dve.wait_ge(self.scored, self.units * b + u + 1)
        dve.tensor_reduce(out=self.neg_max[:, u % 2, :], in_=self.scores(u), axis=X_AXIS, op=ALU.max,
                          negate=True).then_inc(self.maxed, 1)

    def normalize(self, dve, b, u):
        tile, g0, s = self.unit(u)
        got = self.psum[:, 6 + u % 2, 0:self.heads * VC].rearrange("p (g j c) -> p g j c", j=2, c=VC)
        inv = self.inv_sum[:, u % 2, :].rearrange("p (g j) -> p g j", j=2)
        dve.wait_ge(self.weighted, self.units * b + u + 1)
        dve.reciprocal(inv, got[:, :, :, DH]).then_inc(self.summed, 1)
        dve.wait_ge(self.summed, self.units * b + u + 1)
        dve.tensor_tensor(self.out[:, tile % 2, g0:g0 + self.chunks, s, :, :], got[:, :, :, 0:DH],
                          inv.unsqueeze(3).to_broadcast([P, self.chunks, 2, DH]), ALU.mult).then_inc(self.normed, 1)

    def vector(self, dve, b):
        self.maxima(dve, b, 0)
        for step in range(self.units + 2):
            if step + 1 < self.units:
                self.maxima(dve, b, step + 1)
            for group in self.groups(step):
                hi, lo = self.destination(group)
                dve.wait_ge(self.flip_hi, len(self.order) * b + self.place[group] + 1)
                dve.tensor_tensor(lo, self.bank(group), hi, ALU.subtract).then_inc(self.flip_lo, 1)
            if 1 <= step <= self.units:
                self.normalize(dve, b, step - 1)



HALF_WIN = 16
QW = P - 2 * HALF_WIN
NW = -(-S // QW)
PADDED = QW * (NW - 1) + P
SQ = PADDED


def window_attention(nc, consts, psum, x_in, x_out, dram):
    stack, sb, sem = scoped(nc)
    with stack:
        wq, wk, wv, wo = ([sb(f"wa_w{m}{p}", [P, KC, D], F16) for p in range(2)] for m in "qkvo")
        bias = {m: sb(f"wa_b{m}", [BIAS_P, D], F16) for m in "qkvo"}
        split_weights(nc, "wa", [j for pair, matrix in ((wq, dram["l0_wq"]), (wk, dram["l0_wk"]), (wv, dram["l0_wv"]), (wo, dram["l0_wo"]))
                                 for j in square_jobs(pair, matrix)],
                      [(bias["q"][:, :], dram["l0_bq"]), (bias["k"][:, :], dram["l0_bk"]), (bias["v"][:, :], dram["l0_bv"]), (bias["o"][:, :], dram["l0_bo"])])

        n = Norm(nc, sb, sem, "wa", consts, psum, width=PADDED, first=HALF_WIN)
        valid = sb("wa_valid", [BIAS_P, PADDED], F16)
        mask = sb("wa_mask", [P, P], BF16)
        qt = [sb(f"wa_qt{p}", [P, KC, SQ], F16) for p in range(2)]
        kt = [sb(f"wa_kt{p}", [P, KC, PADDED], F16) for p in range(2)]
        v = [sb(f"wa_v{p}", [P, NW, H, VC], F16) for p in range(2)]
        ot = [sb(f"wa_ot{p}", [P, KC, SQ], F16) for p in range(2)]
        ready = sem("wa_ready")
        mask_filled = sem("wa_mask_filled")
        projected, proj_hi, proj_lo = sem("wa_projected"), sem("wa_proj_hi"), sem("wa_proj_lo")
        local = LocalHeads(nc, sb, sem, "wa", consts, psum, NW, QW, 1, mask, qt, kt, v, ot)
        o = OutProjection(ot=ot, wo=wo, bias=bias["o"][:, :], projected=sem("wa_out_projected"))

        qscale = 1.0 / (WS * DH ** 0.5)
        QK_ITEMS = 2 * KC * 2
        ITEMS = QK_ITEMS + NW
        real_cols = slice(HALF_WIN, HALF_WIN + S)

        def item(i):
            if i < QK_ITEMS:
                m, half = (i % (2 * KC)) // 2, i % 2
                first = half * 512 + (HALF_WIN if i >= QK_ITEMS // 2 else 0)
                out = qt if i < QK_ITEMS // 2 else kt
                return [out[p][:, m, first:first + 512] for p in range(2)], \
                    psum[:, i % 4, :], (qscale if i < QK_ITEMS // 2 else 1 / WS)
            return [v[p][:, i - QK_ITEMS, :, 0:DH] for p in range(2)], \
                psum[:, i % 4, :].rearrange("p (h d) -> p h d", d=DH), 1 / WS

        with nc.Block() as block:
            @block.sync
            def _(sp):
                stream_rows(sp, n, x_in, x_out)

            @block.gpsimd
            def _(pool):
                for part in range(2):
                    for edge in (slice(0, HALF_WIN), slice(HALF_WIN + S, PADDED)):
                        pool.memset(n.xt[part][:, :, edge], 0.0)
                        pool.memset(kt[part][:, :, edge], 0.0)
                    pool.memset(qt[part][:, :, S:SQ], 0.0)
                    pool.memset(local.pt[part][:, :, :, :, QW:P], 1.0)
                pool.memset(v[0][:, :, :, :], 1.0)
                pool.memset(v[1][:, :, :, :], 0.0)
                pool.memset(valid[:, :], 0.0).then_inc(mask_filled, 1)
                pool.memset(mask[:, :], 0.0).then_inc(mask_filled, 1)
                pool.wait_ge(mask_filled, 2)
                pool.memset(valid[:, real_cols], 1.0)
                pool.affine_select(out=mask[:, :], in_=mask[:, :], compare_op=ALU.is_ge, fill=MASKED, base=0,
                                   pattern=[[1, P]], channel_multiplier=-1).then_inc(mask_filled, 1)
                pool.wait_ge(mask_filled, 3)
                pool.affine_select(out=mask[:, :], in_=mask[:, :], compare_op=ALU.is_ge, fill=MASKED,
                                   base=2 * HALF_WIN, pattern=[[-1, P]], channel_multiplier=1).then_inc(ready, 1)
                with pool.Fori(0, B) as b:
                    norm_gpsimd(pool, n, b)

            @block.tensor
            def _(pe):
                pe.wait_ge(ready, 1)

                def project(b, i):
                    if i >= 4:
                        pe.wait_ge(proj_lo, ITEMS * b + i - 3)
                    bank = psum[:, i % 4, :]
                    if i < QK_ITEMS:
                        m, half = (i % (2 * KC)) // 2, i % 2
                        wt, bw = (wq, bias["q"]) if i < QK_ITEMS // 2 else (wk, bias["k"])
                        cols = slice(HALF_WIN + half * 512, HALF_WIN + half * 512 + 512)
                        for k in range(KC):
                            for p, q in TERMS:
                                pe.matmul(bank, wt[p][:, k, m * P:(m + 1) * P], n.xt[q][:, k, cols],
                                          start=(k == 0 and (p, q) == (0, 0)), stop=False)
                        pe.matmul(bank, bw[:, m * P:(m + 1) * P], consts.ones[:, 0:512],
                                  start=False, stop=True).then_inc(projected, 1)
                    else:
                        win = i - QK_ITEMS
                        cols = slice(win * QW, win * QW + P)
                        for k in range(KC):
                            for p, q in TERMS:
                                pe.matmul(bank, n.xt[p][:, k, cols], wv[q][:, k, :],
                                          start=(k == 0 and (p, q) == (0, 0)), stop=False)
                        pe.matmul(bank, valid[:, cols], bias["v"][:, :],
                                  start=False, stop=True).then_inc(projected, 1)

                with pe.Fori(0, B) as b:
                    norm_tensor(pe, n, b)
                    pe.wait_ge(n.xt_lo, NT * (b + 1))
                    for i in range(ITEMS):
                        project(b, i)
                    pe.wait_ge(proj_lo, ITEMS * (b + 1))
                    local.tensor(pe, b)
                    out_projection_tensor(pe, n, o, b)

            @block.scalar
            def _(act):
                with act.Fori(0, B) as b:
                    norm_scalar(act, n, b)
                    for i in range(ITEMS):
                        out, bank, scale = item(i)
                        act.wait_ge(projected, ITEMS * b + i + 1)
                        act.activation(out[0], bank, ACT.Copy, scale=scale).then_inc(proj_hi, 1)
                    local.scalar(act, b)

            @block.vector
            def _(dve):
                with dve.Fori(0, B) as b:
                    norm_vector(dve, n, b)
                    for i in range(ITEMS):
                        out, bank, scale = item(i)
                        dve.wait_ge(proj_hi, ITEMS * b + i + 1)
                        dve.scalar_tensor_tensor(out=out[1], in0=bank, scalar=scale, in1=out[0],
                                                 op0=ALU.mult, op1=ALU.subtract).then_inc(proj_lo, 1)
                    local.vector(dve, b)
                    out_projection_vector(dve, n, o, b)



def block_attention(nc, consts, psum, x_in, x_out, dram):
    stack, sb, sem = scoped(nc)
    with stack:
        wo = [sb(f"ba_wo{p}", [P, KC, D], F16) for p in range(2)]
        bias = sb("ba_bo", [BIAS_P, D], F16)
        split_weights(nc, "ba", square_jobs(wo, dram["l0_xo"]), [(bias[:, :], dram["l0_xbo"])])

        n = Norm(nc, sb, sem, "ba", consts, psum, scale=DH ** -0.5)
        qt = n.xt
        mask = sb("ba_mask", [P, P], BF16)
        kt_stage, v_stage = sb("ba_kt_stage", [P, KC, S], F32), sb("ba_v_stage", [P, NT, D], F32)
        kt = [sb(f"ba_kt{p}", [P, KC, S], F16) for p in range(2)]
        v = [sb(f"ba_v{p}", [P, NT, H, VC], F16) for p in range(2)]
        ot = [sb(f"ba_ot{p}", [P, KC, S], F16) for p in range(2)]
        ready, mask_filled = sem("ba_ready"), sem("ba_mask_filled")
        ctx_loaded, ctx_hi, ctx_lo = sem("ba_ctx_loaded"), sem("ba_ctx_hi"), sem("ba_ctx_lo")
        kept = sem("ba_kept")
        local = LocalHeads(nc, sb, sem, "ba", consts, psum, NT, P, 2, mask, qt, kt, v, ot)
        o = OutProjection(ot=ot, wo=wo, bias=bias[:, :], projected=sem("ba_out_projected"))

        splits = [(kt[0][:, k, :], kt[1][:, k, :], kt_stage[:, k, :]) for k in range(KC)] + \
            [(v[0][:, t, :, 0:DH], v[1][:, t, :, 0:DH],
              v_stage[:, t, :].rearrange("p (h d) -> p h d", d=DH)) for t in range(NT)]

        with nc.Block() as block:
            @block.sync
            def _(sp):
                def load_context(b):
                    sp.dma_start(kt_stage[:, :, :], dram["ctx_t"][bass.ds(b * D, D), :]
                                 .rearrange("(k p) s -> p k s", p=P)).then_inc(ctx_loaded, 16)
                    sp.dma_start(v_stage[:, :, :], dram["ctx"][bass.ds(b * S, S), :]
                                 .rearrange("(t p) d -> p t d", p=P)).then_inc(ctx_loaded, 16)

                def keep_context(b):
                    sp.wait_ge(ctx_lo, len(splits) * (b + 1))
                    for p in range(2):
                        sp.dma_start(dram["ctx_parts"][p][bass.ds(b * P, P), :],
                                     kt[p][:, :, :].rearrange("p k s -> p (k s)")).then_inc(kept, 16)
                    sp.wait_ge(kept, 32 * (b + 1))

                def between(b):
                    keep_context(b)
                    load_context(b + 1)

                load_context(0)
                stream_rows(sp, n, x_in, x_out, between)
                keep_context(B - 1)

            @block.gpsimd
            def _(pool):
                pool.memset(v[0][:, :, :, :], 1.0).then_inc(ready, 1)
                pool.memset(v[1][:, :, :, :], 0.0).then_inc(ready, 1)
                pool.memset(mask[:, :], 0.0).then_inc(mask_filled, 1)
                pool.wait_ge(mask_filled, 1)
                pool.affine_select(out=mask[:, :], in_=mask[:, :], compare_op=ALU.is_ge, fill=MASKED, base=0,
                                   pattern=[[-1, P]], channel_multiplier=1).then_inc(ready, 1)
                with pool.Fori(0, B) as b:
                    norm_gpsimd(pool, n, b)

            @block.tensor
            def _(pe):
                pe.wait_ge(ready, 3)

                with pe.Fori(0, B) as b:
                    norm_tensor(pe, n, b)
                    pe.wait_ge(n.xt_lo, NT * (b + 1))
                    pe.wait_ge(ctx_lo, len(splits) * (b + 1))
                    local.tensor(pe, b)
                    out_projection_tensor(pe, n, o, b)

            @block.scalar
            def _(act):
                act.wait_ge(ready, 3)
                with act.Fori(0, B) as b:
                    act.wait_ge(ctx_loaded, 32 * (b + 1))
                    for hi, _, full in splits:
                        act.activation(hi, full, ACT.Copy).then_inc(ctx_hi, 1)
                    norm_scalar(act, n, b)
                    local.scalar(act, b)

            @block.vector
            def _(dve):
                with dve.Fori(0, B) as b:
                    for i, (hi, lo, full) in enumerate(splits):
                        dve.wait_ge(ctx_hi, len(splits) * b + i + 1)
                        dve.tensor_tensor(lo, full, hi, ALU.subtract).then_inc(ctx_lo, 1)
                    norm_vector(dve, n, b)
                    local.vector(dve, b)
                    out_projection_vector(dve, n, o, b)



E = 8
R = 16
TOP_K = 2


def expert_ffn(nc, consts, psum, x_in, x_out, dram):
    stack, sb, sem = scoped(nc)
    with stack:
        GA = E + E * R
        wga = [sb(f"ef_wga{p}", [P, KC, GA], F16) for p in range(2)]
        wb = [sb(f"ef_wb{p}", [P, 1, D], F16) for p in range(2)]
        view = lambda a: a.rearrange("(k p) n -> p k n", p=P)
        split_weights(nc, "ef", [
            (wga[0][:, :, 0:E], wga[1][:, :, 0:E], view(dram["l0_g"])),
            (wga[0][:, :, E:GA], wga[1][:, :, E:GA], view(dram["l0_a"])),
            (wb[0][:, :, :], wb[1][:, :, :], view(dram["l0_b"]))])

        n = Norm(nc, sb, sem, "ef", consts, psum)
        gh = sb("ef_gh", [P, NT, GA], F32)
        logits, hidden = gh[:, :, 0:E], gh[:, :, E:GA].rearrange("p t (e r) -> p t e r", r=R)
        before = sb("ef_before", [P, E, E], F32)
        larger, equal = sb("ef_larger", [P, NT, E, E], F32), sb("ef_equal", [P, NT, E, E], F32)
        rank, chosen = sb("ef_rank", [P, NT, E], F32), sb("ef_chosen", [P, NT, E], F32)
        top, total = sb("ef_top", [P, NT], F32), sb("ef_total", [P, NT], F32)
        share = sb("ef_share", [P, NT, E], F32)
        hw = sb("ef_hw", [P, NT, E, R], F32)
        hwt = [sb(f"ef_hwt{p}", [P, 1, S], F16) for p in range(2)]
        before_filled = sem("ef_before_filled")
        projected, gathered = sem("ef_projected"), sem("ef_gathered")
        gate_step, shifted, exped = sem("ef_gate_step"), sem("ef_shifted"), sem("ef_exped")
        weighed = sem("ef_weighed")
        flipped, flip_hi, flip_lo = sem("ef_flipped"), sem("ef_flip_hi"), sem("ef_flip_lo")
        o = OutProjection(ot=hwt, wo=wb, bias=None, projected=sem("ef_out_projected"))
        FLIPS, GATE_STEPS = 2, 11
        per_expert = [P, NT, E]

        with nc.Block() as block:
            @block.sync
            def _(sp):
                stream_rows(sp, n, x_in, x_out)

            @block.gpsimd
            def _(pool):
                pool.memset(before[:, :, :], 1.0).then_inc(before_filled, 1)
                pool.wait_ge(before_filled, 1)
                pool.affine_select(out=before[:, :, :], in_=before[:, :, :], compare_op=ALU.is_gt, fill=0.0, base=0,
                                   pattern=[[1, E], [-1, E]], channel_multiplier=0).then_inc(before_filled, 1)
                with pool.Fori(0, B) as b:
                    norm_gpsimd(pool, n, b)

            @block.tensor
            def _(pe):
                with pe.Fori(0, B) as b:
                    norm_tensor(pe, n, b)
                    for t in range(NT):
                        pe.wait_ge(n.xt_lo, NT * b + t + 1)
                        if t >= 4:
                            pe.wait_ge(gathered, NT * b + t - 3)
                        for i, (k, (p, q)) in enumerate((k, term) for k in range(KC) for term in TERMS):
                            last = pe.matmul(psum[:, t % 4, 0:GA], n.xt[p][:, k, t * P:(t + 1) * P],
                                             wga[q][:, k, :], start=(i == 0), stop=(i == 3 * KC - 1))
                        last.then_inc(projected, 1)
                    pe.wait_ge(weighed, b + 1)
                    for f in range(FLIPS):
                        for i in range(4):
                            last = pe.transpose(psum[:, 4 + f, i * P:(i + 1) * P],
                                                hw[:, 4 * f + i, :, :].rearrange("p e r -> p (e r)"),
                                                consts.ident[:, :])
                        last.then_inc(flipped, 1)
                    pe.wait_ge(flip_lo, FLIPS * (b + 1))
                    out_projection_tensor(pe, n, o, b)

            @block.scalar
            def _(act):
                with act.Fori(0, B) as b:
                    norm_scalar(act, n, b)
                    for t in range(NT):
                        act.wait_ge(projected, NT * b + t + 1)
                        act.activation(gh[:, t, :], psum[:, t % 4, 0:GA], ACT.Copy, scale=1 / WS).then_inc(gathered, 1)
                    act.wait_ge(shifted, b + 1)
                    act.activation(share[:, :, :], share[:, :, :], ACT.Exp).then_inc(exped, 1)
                    for f in range(FLIPS):
                        act.wait_ge(flipped, FLIPS * b + f + 1)
                        act.activation(hwt[0][:, 0, f * 512:(f + 1) * 512], psum[:, 4 + f, :],
                                       ACT.Copy).then_inc(flip_hi, 1)

            @block.vector
            def _(dve):
                dve.wait_ge(before_filled, 2)
                with dve.Fori(0, B) as b:
                    norm_vector(dve, n, b)
                    done = lambda k: GATE_STEPS * b + k
                    dve.wait_ge(gathered, NT * (b + 1))
                    dve.tensor_reduce(out=top[:, :], in_=logits, axis=X_AXIS, op=ALU.max).then_inc(gate_step, 1)
                    dve.tensor_tensor(larger[:, :, :, :], logits.unsqueeze(2).to_broadcast([P, NT, E, E]),
                                      logits.unsqueeze(3).to_broadcast([P, NT, E, E]), ALU.is_gt).then_inc(gate_step, 1)
                    dve.tensor_tensor(equal[:, :, :, :], logits.unsqueeze(2).to_broadcast([P, NT, E, E]),
                                      logits.unsqueeze(3).to_broadcast([P, NT, E, E]),
                                      ALU.is_equal).then_inc(gate_step, 1)
                    dve.wait_ge(gate_step, done(1))
                    dve.tensor_tensor(share[:, :, :], logits, top[:, :].unsqueeze(2).to_broadcast(per_expert),
                                      ALU.subtract).then_inc(shifted, 1)
                    dve.wait_ge(gate_step, done(3))
                    dve.tensor_tensor(equal[:, :, :, :], equal[:, :, :, :],
                                      before[:, :, :].unsqueeze(1).to_broadcast([P, NT, E, E]),
                                      ALU.mult).then_inc(gate_step, 1)
                    dve.wait_ge(gate_step, done(4))
                    dve.tensor_tensor(larger[:, :, :, :], larger[:, :, :, :], equal[:, :, :, :],
                                      ALU.add).then_inc(gate_step, 1)
                    dve.wait_ge(gate_step, done(5))
                    dve.tensor_reduce(out=rank[:, :, :], in_=larger[:, :, :, :], axis=X_AXIS,
                                      op=ALU.add).then_inc(gate_step, 1)
                    dve.wait_ge(gate_step, done(6))
                    dve.tensor_scalar(chosen[:, :, :], rank[:, :, :], TOP_K - 0.5, None, ALU.is_lt).then_inc(gate_step, 1)
                    dve.wait_ge(gate_step, done(7))
                    dve.wait_ge(exped, b + 1)
                    dve.tensor_tensor(share[:, :, :], share[:, :, :], chosen[:, :, :], ALU.mult).then_inc(gate_step, 1)
                    dve.wait_ge(gate_step, done(8))
                    dve.tensor_reduce(out=total[:, :], in_=share[:, :, :], axis=X_AXIS, op=ALU.add).then_inc(gate_step, 1)
                    dve.wait_ge(gate_step, done(9))
                    dve.reciprocal(total[:, :], total[:, :]).then_inc(gate_step, 1)
                    dve.wait_ge(gate_step, done(10))
                    dve.tensor_tensor(share[:, :, :], share[:, :, :], total[:, :].unsqueeze(2).to_broadcast(per_expert),
                                      ALU.mult).then_inc(gate_step, 1)
                    dve.wait_ge(gate_step, done(11))
                    dve.tensor_tensor(hw[:, :, :, :], hidden, share[:, :, :].unsqueeze(3).to_broadcast([P, NT, E, R]),
                                      ALU.mult).then_inc(weighed, 1)
                    for f in range(FLIPS):
                        cols = slice(f * 512, (f + 1) * 512)
                        dve.wait_ge(flip_hi, FLIPS * b + f + 1)
                        dve.tensor_tensor(hwt[1][:, 0, cols], psum[:, 4 + f, :], hwt[0][:, 0, cols],
                                          ALU.subtract).then_inc(flip_lo, 1)
                    out_projection_vector(dve, n, o, b)



def band_attention(nc, consts, psum, x_in, x_out, dram):
    stack, sb, sem = scoped(nc)
    with stack:
        wq, wk, wv = ([sb(f"bd_w{m}{p}", [P, KC, D], F16) for p in range(2)] for m in "qkv")
        bias = {m: sb(f"bd_b{m}", [BIAS_P, D], F16) for m in "qk"}
        split_weights(nc, "bd", [j for pair, matrix in ((wq, dram["l1_wq"]), (wk, dram["l1_wk"]), (wv, dram["l1_wv"]))
                                 for j in square_jobs(pair, matrix)],
                      [(bias["q"][:, :], dram["l1_bq"]), (bias["k"][:, :], dram["l1_bk"])])

        n = Norm(nc, sb, sem, "bd", consts, psum)
        v_bias = sb("bd_v_bias", [P, D], F32)
        behind, ahead = sb("bd_behind", [P, P], BF16), sb("bd_ahead", [P, P], BF16)
        qt = [sb(f"bd_qt{p}", [P, KC, S], F16) for p in range(2)]
        kt = [sb(f"bd_kt{p}", [P, KC, S], F16) for p in range(2)]
        v = [sb(f"bd_v{p}", [P, NT, D], F16) for p in range(2)]
        probs = sb("bd_probs", [P, 2, 3, P], F32)
        pt = [sb(f"bd_pt{p}", [P, 2, 3, P], F16) for p in range(2)]
        neg_max, total = sb("bd_neg_max", [P, 2], F32), sb("bd_total", [P, 2], F32)
        ready, mask_filled, biased = sem("bd_ready"), sem("bd_mask_filled"), sem("bd_biased")
        v_bias_loaded = sem("bd_v_bias_loaded")
        projected, proj_hi, proj_lo = sem("bd_projected"), sem("bd_proj_hi"), sem("bd_proj_lo")
        scored, maxed, exped = sem("bd_scored"), sem("bd_maxed"), sem("bd_exped")
        flipped, flip_hi, flip_lo = sem("bd_flipped"), sem("bd_flip_hi"), sem("bd_flip_lo")
        weighted, inverted = sem("bd_weighted"), sem("bd_inverted")
        qscale = 1.0 / (WS * D ** 0.5)
        QK = 4 * KC
        ITEMS = QK + NT

        def item(i):
            if i < QK:
                m, half = (i % (2 * KC)) // 2, i % 2
                out = qt if i < QK // 2 else kt
                return [out[p][:, m, half * 512:(half + 1) * 512] for p in range(2)], \
                    (qscale if i < QK // 2 else 1 / WS)
            return [v[p][:, i - QK, :] for p in range(2)], 1 / WS

        def blocks(t):
            return [kb for kb in (t - 1, t, t + 1) if 0 <= kb < NT]

        with nc.Block() as block:
            @block.sync
            def _(sp):
                sp.dma_start(v_bias[:, :], dram["l1_bv"].to_broadcast([P, D])).then_inc(v_bias_loaded, 16)
                stream_rows(sp, n, x_in, x_out)

            @block.gpsimd
            def _(pool):
                pool.memset(behind[:, :], 0.0).then_inc(mask_filled, 1)
                pool.memset(ahead[:, :], 0.0).then_inc(mask_filled, 1)
                pool.wait_ge(mask_filled, 2)
                pool.affine_select(out=behind[:, :], in_=behind[:, :], compare_op=ALU.is_ge, fill=MASKED, base=0,
                                   pattern=[[1, P]], channel_multiplier=-1).then_inc(ready, 1)
                pool.affine_select(out=ahead[:, :], in_=ahead[:, :], compare_op=ALU.is_ge, fill=MASKED, base=0,
                                   pattern=[[-1, P]], channel_multiplier=1).then_inc(ready, 1)
                pool.wait_ge(v_bias_loaded, 16)
                with pool.Fori(0, B) as b:
                    norm_gpsimd(pool, n, b)
                    for t in range(NT):
                        pool.wait_ge(n.xn_ready, NT * b + t + 1)
                        pool.tensor_tensor(n.x[:, t, :], n.x[:, t, :], v_bias[:, :], ALU.add).then_inc(biased, 1)

            @block.tensor
            def _(pe):
                pe.wait_ge(ready, 2)

                def project(b, i):
                    if i >= 4:
                        pe.wait_ge(proj_lo, ITEMS * b + i - 3)
                    bank = psum[:, i % 4, :]
                    terms = [(k, p, q) for k in range(KC) for p, q in TERMS]
                    if i < QK:
                        m, half = (i % (2 * KC)) // 2, i % 2
                        wt, bw = (wq, bias["q"]) if i < QK // 2 else (wk, bias["k"])
                        cols = slice(half * 512, (half + 1) * 512)
                        for k, p, q in terms:
                            pe.matmul(bank, wt[p][:, k, m * P:(m + 1) * P], n.xt[q][:, k, cols],
                                      start=((k, p, q) == terms[0]), stop=False)
                        pe.matmul(bank, bw[:, m * P:(m + 1) * P], consts.ones[:, 0:512],
                                  start=False, stop=True).then_inc(projected, 1)
                    else:
                        cols = slice((i - QK) * P, (i - QK + 1) * P)
                        for k, p, q in terms:
                            last = pe.matmul(bank, n.xt[p][:, k, cols], wv[q][:, k, :],
                                             start=((k, p, q) == terms[0]), stop=((k, p, q) == terms[-1]))
                        last.then_inc(projected, 1)

                def score(t):
                    kbs = blocks(t)
                    bank = psum[:, t % 2, :]
                    cols = slice(kbs[0] * P, (kbs[-1] + 1) * P)
                    for k in range(KC):
                        for p, q in TERMS:
                            if (k, p, q) == (KC - 1, *TERMS[-1]):
                                for kb, m in ((t - 1, behind), (t + 1, ahead)):
                                    if kb in kbs:
                                        at = kbs.index(kb) * P
                                        pe.matmul(bank[:, at:at + P], consts.ident_b[:, :], m[:, :],
                                                  start=False, stop=False)
                            last = pe.matmul(bank[:, 0:len(kbs) * P], qt[p][:, k, t * P:(t + 1) * P],
                                             kt[q][:, k, cols], start=(k == 0 and (p, q) == (0, 0)),
                                             stop=(k == KC - 1 and (p, q) == TERMS[-1]))
                    last.then_inc(scored, 1)

                def flip(b, t):
                    pe.wait_ge(exped, NT * b + t + 1)
                    for i in range(len(blocks(t))):
                        last = pe.transpose(psum[:, 2 + t % 2, i * P:(i + 1) * P], probs[:, t % 2, i, :],
                                            consts.ident[:, :])
                    last.then_inc(flipped, 1)

                def weigh(b, t):
                    pe.wait_ge(flip_lo, NT * b + t + 1)
                    if t >= 2:
                        pe.wait_ge(n.res_ready, NT * b + t - 1)
                    terms = [(i, kb, p, q) for i, kb in enumerate(blocks(t)) for p, q in TERMS]
                    for i, kb, p, q in terms:
                        last = pe.matmul(psum[:, 4 + t % 2, :], pt[p][:, t % 2, i, :], v[q][:, kb, :],
                                         start=((i, kb, p, q) == terms[0]), stop=((i, kb, p, q) == terms[-1]))
                    last.then_inc(weighted, 1)

                with pe.Fori(0, B) as b:
                    norm_tensor(pe, n, b)
                    pe.wait_ge(n.xt_lo, NT * (b + 1))
                    for i in range(ITEMS):
                        project(b, i)
                    pe.wait_ge(proj_lo, ITEMS * (b + 1))
                    score(0)
                    for t in range(NT):
                        if t + 1 < NT:
                            score(t + 1)
                        flip(b, t)
                        if t >= 1:
                            weigh(b, t - 1)
                    weigh(b, NT - 1)

            @block.scalar
            def _(act):
                with act.Fori(0, B) as b:
                    norm_scalar(act, n, b)
                    for i in range(ITEMS):
                        out, scale = item(i)
                        act.wait_ge(projected, ITEMS * b + i + 1)
                        act.activation(out[0], psum[:, i % 4, :], ACT.Copy, scale=scale).then_inc(proj_hi, 1)
                    for t in range(NT):
                        m = len(blocks(t))
                        act.wait_ge(maxed, NT * b + t + 1)
                        act.activation(probs[:, t % 2, 0:m, :],
                                       psum[:, t % 2, 0:m * P].rearrange("p (i c) -> p i c", c=P), ACT.Exp,
                                       bias=neg_max[:, t % 2:t % 2 + 1],
                                       accum_out=total[:, t % 2:t % 2 + 1]).then_inc(exped, 1)
                        act.wait_ge(flipped, NT * b + t + 1)
                        act.activation(pt[0][:, t % 2, 0:m, :],
                                       psum[:, 2 + t % 2, 0:m * P].rearrange("p (i c) -> p i c", c=P),
                                       ACT.Copy).then_inc(flip_hi, 1)

            @block.vector
            def _(dve):
                def maxima(b, t):
                    dve.wait_ge(scored, NT * b + t + 1)
                    dve.tensor_reduce(out=neg_max[:, t % 2:t % 2 + 1], in_=psum[:, t % 2, 0:len(blocks(t)) * P],
                                      axis=X_AXIS, op=ALU.max, negate=True).then_inc(maxed, 1)

                def residual(b, t):
                    dve.wait_ge(weighted, NT * b + t + 1)
                    dve.wait_ge(biased, NT * b + t + 1)
                    dve.scalar_tensor_tensor(out=n.x[:, t, :], in0=psum[:, 4 + t % 2, :],
                                             scalar=total[:, t % 2:t % 2 + 1], in1=n.x[:, t, :],
                                             op0=ALU.mult, op1=ALU.add).then_inc(n.res_ready, 1)

                with dve.Fori(0, B) as b:
                    norm_vector(dve, n, b)
                    for i in range(ITEMS):
                        out, scale = item(i)
                        dve.wait_ge(proj_hi, ITEMS * b + i + 1)
                        dve.scalar_tensor_tensor(out=out[1], in0=psum[:, i % 4, :], scalar=scale, in1=out[0],
                                                 op0=ALU.mult, op1=ALU.subtract).then_inc(proj_lo, 1)
                    maxima(b, 0)
                    for t in range(NT):
                        m = len(blocks(t))
                        if t >= 1:
                            residual(b, t - 1)
                        if t + 1 < NT:
                            maxima(b, t + 1)
                        dve.wait_ge(exped, NT * b + t + 1)
                        dve.reciprocal(total[:, t % 2:t % 2 + 1], total[:, t % 2:t % 2 + 1]).then_inc(inverted, 1)
                        dve.wait_ge(flip_hi, NT * b + t + 1)
                        dve.tensor_tensor(pt[1][:, t % 2, 0:m, :],
                                          psum[:, 2 + t % 2, 0:m * P].rearrange("p (i c) -> p i c", c=P),
                                          pt[0][:, t % 2, 0:m, :], ALU.subtract).then_inc(flip_lo, 1)
                    dve.wait_ge(inverted, NT * (b + 1))
                    residual(b, NT - 1)



HX = 16
DX = 64
PAIRS = HX // 2
HALF = 512


def cross_attention(nc, consts, psum, x_in, x_out, dram):
    stack, sb, sem = scoped(nc)
    with stack:
        WIDE = HX * DX
        wq, wk, wv = ([sb(f"ca_w{m}{p}", [P, KC, WIDE], F16) for p in range(2)] for m in "qkv")
        wo = [sb(f"ca_wo{p}", [P, PAIRS, D], F16) for p in range(2)]
        split_weights(nc, "ca", [j for pair, matrix, cols in ((wq, dram["l1_xq"], WIDE), (wk, dram["l1_xk"], WIDE), (wv, dram["l1_xv"], WIDE),
                                                            (wo, dram["l1_xo"], D))
                                 for j in square_jobs(pair, matrix, cols)])

        n = Norm(nc, sb, sem, "ca", consts, psum)
        ct = [sb(f"ca_ct{p}", [P, KC, S], F16) for p in range(2)]
        qt = [[sb(f"ca_qt{a}{p}", [P, S], F16) for p in range(2)] for a in range(2)]
        kt = [[sb(f"ca_kt{a}{p}", [P, S], F16) for p in range(2)] for a in range(2)]
        v = [[sb(f"ca_v{a}{p}", [P, NT, 2 * DX], F16) for p in range(2)] for a in range(2)]
        probs = sb("ca_probs", [P, 2, S], F32)
        pt = [sb(f"ca_pt{p}", [P, 2, NT, P], F16) for p in range(2)]
        neg_max = sb("ca_neg_max", [P, 2, 2], F32)
        total = sb("ca_total", [P, 2, 2], F32)
        pair_out = sb("ca_pair_out", [P, 4, 2, DX], F32)
        ot = [sb(f"ca_ot{p}", [P, PAIRS, S], F16) for p in range(2)]
        ct_loaded = sem("ca_ct_loaded")
        projected, proj_hi, proj_lo = sem("ca_projected"), sem("ca_proj_hi"), sem("ca_proj_lo")
        scored, maxed, exped = sem("ca_scored"), sem("ca_maxed"), sem("ca_exped")
        flipped, flip_hi, flip_lo = sem("ca_flipped"), sem("ca_flip_hi"), sem("ca_flip_lo")
        weighted, inverted, normed = sem("ca_weighted"), sem("ca_inverted"), sem("ca_normed")
        o = OutProjection(ot=ot, wo=wo, bias=None, projected=sem("ca_out_projected"))
        qscale = 1.0 / (WS * DX ** 0.5)
        QK = 4
        ITEMS = QK + NT // 2
        STEPS = NT
        FLIPS = 4 * STEPS + 2

        def flip_at(t, i):
            return 4 * t + i + (1 if t >= 4 else 0)

        def item(a, i):
            if i < QK:
                out = qt[a] if i < 2 else kt[a]
                return [out[p][:, (i % 2) * HALF:(i % 2 + 1) * HALF] for p in range(2)], \
                    psum[:, 7, :], (qscale if i < 2 else 1 / WS)
            t = 2 * (i - QK)
            return [v[a][p][:, t:t + 2, :] for p in range(2)], \
                psum[:, 7, 0:4 * DX].rearrange("p (t c) -> p t c", c=2 * DX), 1 / WS

        def flip_bank(f):
            return psum[:, 4 + f % 2, :]

        def pairs(e, body):
            with e.Fori(0, PAIRS // 2 - 1) as twice:
                for a in range(2):
                    body(twice * 2 + a, a, True)
            for a in range(2):
                body(PAIRS - 2 + a, a, a == 0)

        with nc.Block() as block:
            @block.sync
            def _(sp):
                def load_context(b):
                    for p in range(2):
                        sp.dma_start(ct[p][:, :, :].rearrange("p k s -> p (k s)"),
                                     dram["ctx_parts"][p][bass.ds(b * P, P), :]).then_inc(ct_loaded, 16)

                def between(b):
                    sp.wait_ge(projected, ITEMS * PAIRS * (b + 1))
                    load_context(b + 1)

                load_context(0)
                stream_rows(sp, n, x_in, x_out, between)

            @block.gpsimd
            def _(pool):
                with pool.Fori(0, B) as b:
                    norm_gpsimd(pool, n, b)

            @block.tensor
            def _(pe):
                def project(b, pair, a, i):
                    done = ITEMS * PAIRS * b + pair * ITEMS + i
                    if i == 0 and isinstance(pair, int) and pair == 0:
                        pass
                    else:
                        pe.wait_ge(proj_lo, done)
                    feats = bass.ds(pair * P, P)
                    if i < QK:
                        wt, src = (wq, n.xt) if i < 2 else (wk, ct)
                        cols = slice((i % 2) * HALF, (i % 2 + 1) * HALF)
                        for j, (k, (p, q)) in enumerate((k, term) for k in range(KC) for term in TERMS):
                            last = pe.matmul(psum[:, 7, :], wt[p][:, k, feats], src[q][:, k, cols],
                                             start=(j == 0), stop=(j == 3 * KC - 1))
                    else:
                        for s in range(2):
                            t = 2 * (i - QK) + s
                            for j, (k, (p, q)) in enumerate((k, term) for k in range(KC) for term in TERMS):
                                last = pe.matmul(psum[:, 7, s * P:(s + 1) * P], ct[p][:, k, t * P:(t + 1) * P],
                                                 wv[q][:, k, feats], start=(j == 0), stop=(j == 3 * KC - 1))
                    last.then_inc(projected, 1)

                def score(a, t):
                    for half in range(2):
                        for i, (p, q) in enumerate(TERMS):
                            for h in range(2):
                                r = slice(DX * h, DX * (h + 1))
                                last = pe.matmul(psum[:, 2 * h + half, :], qt[a][p][r, t * P:(t + 1) * P],
                                                 kt[a][q][r, half * HALF:(half + 1) * HALF],
                                                 start=(i == 0), stop=(i == 2))
                    last.then_inc(scored, 1)

                def body(b, pair, a, follows):
                    steps = STEPS * PAIRS * b + pair * STEPS
                    flips = FLIPS * PAIRS * b + pair * FLIPS
                    items = ITEMS * PAIRS * b + pair * ITEMS
                    def flip(t, i):
                        f = flip_at(t, i)
                        if f >= 1:
                            pe.wait_ge(flip_lo, 1 + flips + f - 1)
                        if i < 4:
                            h, half = i // 2, i % 2
                            pe.wait_ge(exped, 2 * steps + 2 * t + h + 1)
                            sources = [probs[:, h, kb * P:(kb + 1) * P] for kb in range(4 * half, 4 * half + 4)]
                        else:
                            pe.wait_ge(normed, steps + t + 1)
                            sources = [pair_out[:, c, :, :].rearrange("p h d -> p (h d)") for c in range(4)]
                        for c in range(4):
                            last = pe.transpose(flip_bank(f)[:, c * P:(c + 1) * P], sources[c], consts.ident[:, :])
                        last.then_inc(flipped, 1)

                    def weigh(t, h):
                        pe.wait_ge(flip_lo, 1 + flips + flip_at(t, 2 * h + 1) + 1)
                        terms = [(kb, p, q) for kb in range(NT) for p, q in TERMS]
                        for j, (kb, p, q) in enumerate(terms):
                            last = pe.matmul(psum[:, 6, h * DX:(h + 1) * DX], pt[p][:, h, kb, :],
                                             v[a][q][:, kb, h * DX:(h + 1) * DX],
                                             start=(j == 0), stop=(j == len(terms) - 1))
                        if h == 1:
                            last.then_inc(weighted, 1)

                    for t in range(STEPS):
                        flip(t, 0)
                        flip(t, 1)
                        if t == 0:
                            pe.wait_ge(proj_lo, items + ITEMS)
                        if t + 1 < STEPS or follows:
                            pe.wait_ge(exped, 2 * steps + 2 * t + 2)
                        if t + 1 < STEPS:
                            score(a, t + 1)
                        elif follows:
                            pe.wait_ge(proj_lo, items + ITEMS + QK)
                            score(1 - a, 0)
                        flip(t, 2)
                        flip(t, 3)
                        weigh(t, 0)
                        if follows:
                            project(b, pair + 1, 1 - a, t)
                        weigh(t, 1)
                        if t % 4 == 3:
                            flip(t, 4)

                with pe.Fori(0, B) as b:
                    norm_tensor(pe, n, b)
                    pe.wait_ge(n.xt_lo, NT * (b + 1))
                    pe.wait_ge(ct_loaded, 32 * (b + 1))
                    for i in range(ITEMS):
                        project(b, 0, 0, i)
                    pe.wait_ge(proj_lo, ITEMS * PAIRS * b + QK)
                    score(0, 0)
                    pairs(pe, lambda pair, a, follows: body(b, pair, a, follows))
                    pe.wait_ge(flip_lo, 1 + FLIPS * PAIRS * (b + 1))
                    out_projection_tensor(pe, n, o, b)

            @block.scalar
            def _(act):
                def split_item(b, pair, a, i):
                    out, bank, scale = item(a, i)
                    act.wait_ge(projected, ITEMS * PAIRS * b + pair * ITEMS + i + 1)
                    act.activation(out[0], bank, ACT.Copy, scale=scale).then_inc(proj_hi, 1)

                def exponentials(steps, t):
                    for h in range(2):
                        act.wait_ge(maxed, 2 * steps + 2 * t + h + 1)
                        act.activation(probs[:, h, :], psum[:, 2 * h:2 * h + 2, :].rearrange("p a c -> p (a c)"),
                                       ACT.Exp, bias=neg_max[:, t % 2, h:h + 1],
                                       accum_out=total[:, t % 2, h:h + 1]).then_inc(exped, 1)

                def body(b, pair, a, follows):
                    steps = STEPS * PAIRS * b + pair * STEPS
                    flips = FLIPS * PAIRS * b + pair * FLIPS
                    for t in range(STEPS):
                        for i in range(4):
                            f = flip_at(t, i)
                            h, half = i // 2, i % 2
                            act.wait_ge(flipped, flips + f + 1)
                            act.activation(pt[0][:, h, 4 * half:4 * half + 4, :],
                                           flip_bank(f).rearrange("p (c q) -> p c q", q=P),
                                           ACT.Copy).then_inc(flip_hi, 1)
                        if t + 1 < STEPS or follows:
                            exponentials(steps, t + 1)
                        if follows:
                            split_item(b, pair + 1, 1 - a, t)
                        if t % 4 == 3:
                            act.wait_ge(flipped, flips + flip_at(t, 4) + 1)
                            act.activation(ot[0][:, pair, (t // 4) * HALF:(t // 4 + 1) * HALF] if isinstance(pair, int)
                                           else ot[0][:, bass.ds(pair, 1), (t // 4) * HALF:(t // 4 + 1) * HALF],
                                           flip_bank(flip_at(t, 4)) if isinstance(pair, int)
                                           else flip_bank(flip_at(t, 4)).unsqueeze(1),
                                           ACT.Copy).then_inc(flip_hi, 1)

                with act.Fori(0, B) as b:
                    norm_scalar(act, n, b)
                    for i in range(ITEMS):
                        split_item(b, 0, 0, i)
                    exponentials(STEPS * PAIRS * b, 0)
                    pairs(act, lambda pair, a, follows: body(b, pair, a, follows))

            @block.vector
            def _(dve):
                def split_item(b, pair, a, i):
                    out, bank, scale = item(a, i)
                    dve.wait_ge(proj_hi, ITEMS * PAIRS * b + pair * ITEMS + i + 1)
                    dve.scalar_tensor_tensor(out=out[1], in0=bank, scalar=scale, in1=out[0],
                                             op0=ALU.mult, op1=ALU.subtract).then_inc(proj_lo, 1)

                def maximum(t, h):
                    dve.tensor_reduce(out=neg_max[:, t % 2, h:h + 1],
                                      in_=psum[:, 2 * h:2 * h + 2, :].rearrange("p a c -> p (a c)"),
                                      axis=X_AXIS, op=ALU.max, negate=True).then_inc(maxed, 1)

                def body(b, pair, a, follows):
                    steps = STEPS * PAIRS * b + pair * STEPS
                    flips = FLIPS * PAIRS * b + pair * FLIPS
                    for t in range(STEPS):
                        def low_parts(i):
                            f, h, half = flip_at(t, i), i // 2, i % 2
                            dve.wait_ge(flip_hi, flips + f + 1)
                            dve.tensor_tensor(pt[1][:, h, 4 * half:4 * half + 4, :],
                                              flip_bank(f).rearrange("p (c q) -> p c q", q=P),
                                              pt[0][:, h, 4 * half:4 * half + 4, :], ALU.subtract).then_inc(flip_lo, 1)

                        low_parts(0)
                        low_parts(1)
                        scores_follow = t + 1 < STEPS or follows
                        if scores_follow:
                            dve.wait_ge(scored, steps + t + 2)
                            maximum(t + 1, 0)
                        low_parts(2)
                        low_parts(3)
                        if scores_follow:
                            maximum(t + 1, 1)
                        dve.reciprocal(total[:, t % 2, :], total[:, t % 2, :]).then_inc(inverted, 1)
                        if follows:
                            split_item(b, pair + 1, 1 - a, t)
                        dve.wait_ge(inverted, steps + t + 1)
                        dve.wait_ge(weighted, steps + t + 1)
                        dve.tensor_tensor(pair_out[:, t % 4, :, :],
                                          psum[:, 6, 0:2 * DX].rearrange("p (h d) -> p h d", d=DX),
                                          total[:, t % 2, :].unsqueeze(2).to_broadcast([P, 2, DX]),
                                          ALU.mult).then_inc(normed, 1)
                        if t % 4 == 3:
                            cols = slice((t // 4) * HALF, (t // 4 + 1) * HALF)
                            dve.wait_ge(flip_hi, flips + flip_at(t, 4) + 1)
                            at = pair if isinstance(pair, int) else bass.ds(pair, 1)
                            src = flip_bank(flip_at(t, 4))
                            dve.tensor_tensor(ot[1][:, at, cols], src if isinstance(pair, int) else src.unsqueeze(1),
                                              ot[0][:, at, cols], ALU.subtract).then_inc(flip_lo, 1)

                dve.memset(n.fence[:, :], 0.0).then_inc(flip_lo, 1)
                with dve.Fori(0, B) as b:
                    norm_vector(dve, n, b)
                    for i in range(ITEMS):
                        split_item(b, 0, 0, i)
                    dve.wait_ge(scored, STEPS * PAIRS * b + 1)
                    for h in range(2):
                        maximum(0, h)
                    pairs(dve, lambda pair, a, follows: body(b, pair, a, follows))
                    out_projection_vector(dve, n, o, b)



FP8_MAX = 448.0
HALVED = 0.5
ROUNDER = 1.5 * 2.0 ** 13
FINE_BELOW = 2.0 ** -6


def fp8_ffn(nc, consts, psum, x_in, x_out, dram):
    stack, sb, sem = scoped(nc)
    with stack:
        weights = sb("ff_weights", [P, KC, D], F16)
        bias, w_scale = sb("ff_bias", [P, D], F32), sb("ff_w_scale", [P, 1], F32)
        n = Norm(nc, sb, sem, "ff", consts, psum, width=2)
        xn = sb("ff_xn_all", [P, NT, D], F32)
        amax, x_scale = sb("ff_amax", [P, NT], F32), sb("ff_x_scale", [P, NT], F32)
        half_inv, out_scale = sb("ff_half_inv", [P, NT], F32), sb("ff_out_scale", [P, NT], F32)
        coarse = sb("ff_coarse", [P, 2, D], F8)
        rounded = sb("ff_rounded", [P, 2, D], F32)
        fine = sb("ff_fine", [P, 2, D], BF16)
        is_fine = sb("ff_is_fine", [P, 2, D], U16)
        q = sb("ff_q", [P, 2, D], BF16)
        qt = sb("ff_qt", [P, KC, S], BF16)
        loaded, decoded = sem("ff_loaded"), sem("ff_decoded")
        biased, scale_step = sem("ff_biased"), sem("ff_scale_step")
        coarsened, widened, added = sem("ff_coarsened"), sem("ff_widened"), sem("ff_added")
        fined, squared, marked, merged = sem("ff_fined"), sem("ff_squared"), sem("ff_marked"), sem("ff_merged")
        flipped, flip_out, projected = sem("ff_flipped"), sem("ff_flip_out"), sem("ff_projected")
        SCALE_STEPS = NT + 3

        decode_stack, dsb, _ = scoped(nc)
        with decode_stack:
            bits8 = dsb("ff_bits8", [P, KC, D], U8)
            bits, sign = dsb("ff_bits", [P, KC, D], U16), dsb("ff_sign", [P, KC, D], U16)
            with nc.Block() as block:
                @block.sync
                def _(sp):
                    sp.dma_start(bits8[:, :, :], dram["l1_w8"].rearrange("(k p) n -> p k n", p=P)).then_inc(loaded, 16)
                    sp.dma_start(bias[:, :], dram["l1_b"].to_broadcast([P, D])).then_inc(loaded, 16)
                    sp.dma_start(w_scale[:, :], dram["l1_s"].to_broadcast([P, 1])).then_inc(loaded, 16)
                    sp.wait_ge(loaded, 48)

                @block.vector
                def _(dve):
                    dve.wait_ge(loaded, 48)
                    dve.tensor_copy(bits[:, :, :], bits8[:, :, :]).then_inc(decoded, 1)
                    dve.wait_ge(decoded, 1)
                    dve.tensor_scalar(sign[:, :, :], bits[:, :, :], 0x80, 8, ALU.bitwise_and,
                                      ALU.logical_shift_left).then_inc(decoded, 1)
                    dve.tensor_scalar(bits[:, :, :], bits[:, :, :], 0x7F, 7, ALU.bitwise_and,
                                      ALU.logical_shift_left).then_inc(decoded, 1)
                    dve.wait_ge(decoded, 3)
                    dve.tensor_tensor(bits[:, :, :], bits[:, :, :], sign[:, :, :], ALU.bitwise_or).then_inc(decoded, 1)
                    dve.wait_ge(decoded, 4)
                    dve.tensor_scalar(weights[:, :, :], bits[:, :, :].bitcast(F16), 2.0 ** 8, None,
                                      ALU.mult).then_inc(decoded, 1)
                    dve.wait_ge(decoded, 5)

        with nc.Block() as block:
            @block.sync
            def _(sp):
                stream_rows(sp, n, x_in, x_out)

            @block.gpsimd
            def _(pool):
                with pool.Fori(0, B) as b:
                    norm_gpsimd(pool, n, b)
                    for t in range(NT):
                        pool.wait_ge(n.xn_ready, NT * b + t + 1)
                        pool.tensor_tensor(n.x[:, t, :], n.x[:, t, :], bias[:, :], ALU.add).then_inc(biased, 1)

            def evacuate(act, b, t):
                act.wait_ge(flipped, NT * b + t + 1)
                act.activation(qt[:, :, t * P:(t + 1) * P],
                               psum[:, 4 + t % 2, 0:256].bitcast(BF16).rearrange("p (k c) -> p k c", c=P),
                               ACT.Copy).then_inc(flip_out, 1)

            @block.scalar
            def _(act):
                with act.Fori(0, B) as b:
                    for t in range(NT):
                        evacuate(act, b, t)

            @block.vector
            def _(dve):
                with dve.Fori(0, B) as b:
                    norm_moments(dve, n, b)
                    for t in range(NT):
                        dve.tensor_scalar(xn[:, t, :], n.x[:, t, :], n.mv[:, t, 0:1], n.rstd[:, t:t + 1],
                                          ALU.subtract, ALU.mult).then_inc(n.xn_ready, 1)
                    for t in range(NT):
                        dve.wait_ge(n.xn_ready, NT * b + t + 1)
                        dve.tensor_reduce(out=amax[:, t:t + 1], in_=xn[:, t, :], axis=X_AXIS, op=ALU.max,
                                          apply_absolute_value=True).then_inc(scale_step, 1)
                    dve.wait_ge(scale_step, SCALE_STEPS * b + NT)
                    dve.tensor_scalar(x_scale[:, :], amax[:, :], 1e-12, 1.0 / FP8_MAX, ALU.max,
                                      ALU.mult).then_inc(scale_step, 1)
                    dve.wait_ge(scale_step, SCALE_STEPS * b + NT + 1)
                    dve.tensor_scalar(out_scale[:, :], x_scale[:, :], w_scale[:, 0:1], 1 / HALVED, ALU.mult, ALU.mult)
                    dve.tensor_scalar(amax[:, :], x_scale[:, :], 1 / HALVED, None, ALU.mult).then_inc(scale_step, 1)
                    dve.wait_ge(scale_step, SCALE_STEPS * b + NT + 2)
                    dve.reciprocal(half_inv[:, :], amax[:, :]).then_inc(scale_step, 1)
                    dve.wait_ge(scale_step, SCALE_STEPS * (b + 1))
                    for t in range(NT):
                        s = t % 2
                        if t >= 2:
                            dve.wait_ge(flipped, NT * b + t - 1)
                        dve.tensor_scalar(rounded[:, s, :], xn[:, t, :], half_inv[:, t:t + 1], ROUNDER,
                                          ALU.mult, ALU.add).then_inc(added, 1)
                        dve.tensor_scalar(coarse[:, s, :], xn[:, t, :], half_inv[:, t:t + 1], None, ALU.mult,
                                          saturate=False).then_inc(coarsened, 1)
                        dve.wait_ge(added, NT * b + t + 1)
                        dve.tensor_scalar(fine[:, s, :], rounded[:, s, :], ROUNDER, None,
                                          ALU.subtract).then_inc(fined, 1)
                        dve.wait_ge(fined, NT * b + t + 1)
                        dve.tensor_tensor(rounded[:, s, :], fine[:, s, :], fine[:, s, :], ALU.mult).then_inc(squared, 1)
                        dve.wait_ge(coarsened, NT * b + t + 1)
                        dve.memset(n.fence[:, :], 0.0)
                        dve.tensor_copy(q[:, s, :], coarse[:, s, :]).then_inc(widened, 1)
                        dve.wait_ge(squared, NT * b + t + 1)
                        dve.tensor_scalar(is_fine[:, s, :], rounded[:, s, :], FINE_BELOW ** 2, None,
                                          ALU.is_lt).then_inc(marked, 1)
                        dve.wait_ge(widened, NT * b + t + 1)
                        dve.wait_ge(marked, NT * b + t + 1)
                        dve.memset(n.fence[:, :], 0.0)
                        dve.copy_predicated(q[:, s, :], is_fine[:, s, :], fine[:, s, :]).then_inc(merged, 1)
                    for t in range(NT):
                        dve.wait_ge(projected, NT * b + t + 1)
                        dve.wait_ge(biased, NT * b + t + 1)
                        dve.scalar_tensor_tensor(out=n.x[:, t, :], in0=psum[:, t % 4, :],
                                                 scalar=out_scale[:, t:t + 1], in1=n.x[:, t, :],
                                                 op0=ALU.mult, op1=ALU.add).then_inc(n.res_ready, 1)

            @block.tensor
            def _(pe):
                def project(b, t):
                    if t >= 4:
                        pe.wait_ge(n.res_ready, NT * b + t - 3)
                    pe.wait_ge(flip_out, NT * b + t + 1)
                    for k in range(KC):
                        last = pe.matmul(psum[:, t % 4, :], qt[:, k, t * P:(t + 1) * P], weights[:, k, :],
                                         start=(k == 0), stop=(k == KC - 1))
                    last.then_inc(projected, 1)

                with pe.Fori(0, B) as b:
                    for t in range(NT):
                        pe.wait_ge(merged, NT * b + t + 1)
                        if t >= 2:
                            pe.wait_ge(flip_out, NT * b + t - 1)
                        for k in range(KC):
                            last = pe.transpose(psum[:, 4 + t % 2, 0:256].bitcast(BF16)[:, k * P:(k + 1) * P],
                                                q[:, t % 2, k * P:(k + 1) * P], consts.ident_b[:, :])
                        last.then_inc(flipped, 1)
                        if t >= 1 and t < 5:
                            project(b, t - 1)
                    for t in range(4, NT):
                        project(b, t)


def program(nc, dram, subs):
    stack, sb, sem = scoped(nc)
    with stack:
        psum = stack.enter_context(nc.psum_tensor("banks", [P, 8, 512], F32))
        consts = constants(nc, sb, sem)
        dram["ctx_parts"] = [nc.dram_tensor(f"ctx_part{p}", (B * P, KC * S), F16, kind="Internal").ap()
                             for p in range(2)]
        x_in = dram["x"]
        for i, name in enumerate(subs):
            consts.turn = i
            x_out = dram["out"] if i == len(subs) - 1 else \
                nc.dram_tensor(f"x_after_{name}", (B * S, D), F32, kind="Internal").ap()
            SUB[name](nc, consts, psum, x_in, x_out, dram)
            x_in = x_out


SUB = {"window_attention": window_attention, "block_attention": block_attention, "expert_ffn": expert_ffn,
       "band_attention": band_attention, "cross_attention": cross_attention, "fp8_ffn": fp8_ffn}
ALL = tuple(SUB)


def kernel(x, ctx_1024, L0_attn_w_qkv, L0_attn_b_qkv, L0_attn_w_out, L0_attn_b_out, L0_xattn_W_out,
           L0_xattn_b_out, L0_ffn_Wg, L0_ffn_A, L0_ffn_B, L1_attn_Wq, L1_attn_bq, L1_attn_Wk, L1_attn_bk,
           L1_attn_Wv, L1_attn_bv, L1_xattn_wq, L1_xattn_wk, L1_xattn_wv, L1_xattn_wo, L1_ffn_weight,
           L1_ffn_weight_scale, L1_ffn_bias):
    import concourse.bacc as bacc
    import numpy as np
    from concourse.bass_utils import run_bass_kernel_spmd

    qkv = np.asarray(L0_attn_w_qkv).reshape(H, 3, DH, D).transpose(1, 3, 0, 2).reshape(3, D, D)
    b_qkv = np.asarray(L0_attn_b_qkv).reshape(H, 3, DH).transpose(1, 0, 2).reshape(3, 1, D)
    arrays = {
        "x": np.asarray(x).reshape(B * S, D),
        "l0_wq": qkv[0], "l0_wk": qkv[1], "l0_wv": qkv[2], "l0_wo": np.asarray(L0_attn_w_out).T,
        "l0_bq": b_qkv[0], "l0_bk": b_qkv[1], "l0_bv": b_qkv[2], "l0_bo": np.asarray(L0_attn_b_out).reshape(1, D),
        "ctx": np.asarray(ctx_1024).reshape(B * S, D),
        "ctx_t": np.asarray(ctx_1024).transpose(0, 2, 1).reshape(B * D, S),
        "l0_xo": np.asarray(L0_xattn_W_out).T, "l0_xbo": np.asarray(L0_xattn_b_out).reshape(1, D),
        "l0_g": np.asarray(L0_ffn_Wg), "l0_a": np.asarray(L0_ffn_A).transpose(1, 0, 2).reshape(D, E * R),
        "l0_b": np.asarray(L0_ffn_B).reshape(E * R, D),
        "l1_wq": np.asarray(L1_attn_Wq), "l1_wk": np.asarray(L1_attn_Wk), "l1_wv": np.asarray(L1_attn_Wv),
        "l1_bq": np.asarray(L1_attn_bq).reshape(1, D), "l1_bk": np.asarray(L1_attn_bk).reshape(1, D),
        "l1_bv": np.asarray(L1_attn_bv).reshape(1, D),
        "l1_xq": np.asarray(L1_xattn_wq).T, "l1_xk": np.asarray(L1_xattn_wk).T, "l1_xv": np.asarray(L1_xattn_wv).T,
        "l1_xo": np.asarray(L1_xattn_wo).T,
        "l1_w8": np.asarray(L1_ffn_weight).view(np.uint8).T, 
        "l1_s": np.asarray(L1_ffn_weight_scale).reshape(1, 1),
        "l1_b": np.asarray(L1_ffn_bias).reshape(1, D),
    }
    arrays = {k: np.ascontiguousarray(a) for k, a in arrays.items()}
    nc = bacc.Bacc("TRN2", target_bir_lowering=False, num_devices=1)
    dram = {k: nc.dram_tensor(f"in_{k}", a.shape, mybir.dt.from_np(a.dtype), kind="ExternalInput").ap()
            for k, a in arrays.items()}
    dram["out"] = nc.dram_tensor("out", (B * S, D), F32, kind="ExternalOutput").ap()
    program(nc, dram, ALL)
    got = run_bass_kernel_spmd(nc, [{f"in_{k}": a for k, a in arrays.items()}], core_ids=[0])
    return got.results[0]["out"].reshape(B, S, D)
```

```python
from contextlib import ExitStack

import concourse.bass as bass
from concourse import mybir

F32 = mybir.dt.float32
F16 = mybir.dt.float16
BF16 = mybir.dt.bfloat16
U8 = mybir.dt.uint8
U16 = mybir.dt.uint16
U32 = mybir.dt.uint32
F8 = mybir.dt.float8e4
ALU = mybir.AluOpType
ACT = mybir.ActivationFunctionType
X_AXIS = mybir.AxisListType.X

B = 4
S = 1024
D = 512
P = 128
NT = S // P
KC = D // P
EPS = 1e-5
WS = 64.0
BIAS_LO = 32
BIAS_P = BIAS_LO + 1
MASKED = -1e30

TERMS = ((0, 0), (0, 1), (1, 0))


def tokens_in(ap, b, t):
    return ap[bass.ds(b * S + t * P, P), :]


def scoped(nc):
    stack, sems = ExitStack(), []

    def clear():
        if sems:
            nc.clear_and_free_semaphores(sems)
            nc.all_engine_barrier()

    def sem(name):
        sems.append(nc.alloc_semaphore(name=name))
        return sems[-1]

    stack.callback(clear)
    sb = lambda name, shape, dt: stack.enter_context(nc.sbuf_tensor(name, shape, dt))
    return stack, sb, sem


class Constants:

    def __init__(self, sb, sem):
        self.ident, self.ident_b = sb("ident", [P, P], F32), sb("ident_b", [P, P], BF16)
        self.ones = sb("ones", [BIAS_P, 512], F16)
        self.minus_half, self.eps = sb("minus_half", [P, NT], F32), sb("eps", [P, NT], F32)
        self.x_loaded = [sem(f"x_loaded{t}") for t in range(NT)]
        self.stored = [sem(f"stored{t}") for t in range(NT)]
        self.turn = 0


def constants(nc, sb, sem):
    c = Constants(sb, sem)
    filled = sem("const_filled")
    with nc.Block() as block:
        @block.gpsimd
        def _(pool):
            pool.memset(c.ident[:, :], 0.0).then_inc(filled, 1)
            pool.memset(c.ident_b[:, :], 0.0).then_inc(filled, 1)
            pool.memset(c.ones[:, :], 1.0).then_inc(filled, 1)
            pool.memset(c.minus_half[:, :], -0.5).then_inc(filled, 1)
            pool.memset(c.eps[:, :], EPS).then_inc(filled, 1)
            pool.wait_ge(filled, 5)
            for m in (c.ident, c.ident_b):
                pool.affine_select(out=m[:, :], in_=m[:, :], compare_op=ALU.not_equal, fill=1.0, base=0,
                                   pattern=[[-1, P]], channel_multiplier=1).then_inc(filled, 1)
            pool.wait_ge(filled, 7)
    return c


def split_weights(nc, tag, jobs, biases=()):
    stack, sb, sem = scoped(nc)
    with stack:
        stage = sb(f"{tag}_stage", [P, 4, 2048], F32)
        bias_stage = sb(f"{tag}_bias_stage", [BIAS_P, max(1, len(biases)), D], F32)
        loaded = [sem(f"{tag}_w_loaded{i}") for i in range(4)]
        bias_zeroed, bias_loaded = sem(f"{tag}_bias_zeroed"), sem(f"{tag}_bias_loaded")
        hi_ready, lo_ready, bias_hi = sem(f"{tag}_w_hi"), sem(f"{tag}_w_lo"), sem(f"{tag}_bias_hi")

        def staged(i):
            k, n = jobs[i][0].shape[1:]
            return stage[:, i % 4, 0:k * n].rearrange("p (k n) -> p k n", n=n)

        with nc.Block() as block:
            @block.sync
            def _(sp):
                for i, (_, _, dram) in enumerate(jobs):
                    if i >= 4:
                        sp.wait_ge(lo_ready, i - 3)
                    sp.dma_start(staged(i), dram).then_inc(loaded[i % 4], 16)
                if biases:
                    sp.wait_ge(bias_zeroed, 1)
                    for i, (_, dram) in enumerate(biases):
                        for p in (0, BIAS_LO):
                            sp.dma_start(bias_stage[p:p + 1, i, :], dram).then_inc(bias_loaded, 16)

            @block.scalar
            def _(act):
                for i, (hi, _, _) in enumerate(jobs):
                    act.wait_ge(loaded[i % 4], 16 * (i // 4 + 1))
                    act.activation(hi, staged(i), ACT.Copy, scale=WS).then_inc(hi_ready, 1)
                if biases:
                    act.wait_ge(bias_loaded, 32 * len(biases))
                    for i, (rows, _) in enumerate(biases):
                        act.activation(rows, bias_stage[:, i, :], ACT.Copy, scale=WS).then_inc(bias_hi, 1)

            @block.vector
            def _(dve):
                if biases:
                    dve.memset(bias_stage[:, :, :], 0.0).then_inc(bias_zeroed, 1)
                for i, (hi, lo, _) in enumerate(jobs):
                    dve.wait_ge(hi_ready, i + 1)
                    dve.scalar_tensor_tensor(out=lo, in0=staged(i), scalar=WS, in1=hi,
                                             op0=ALU.mult, op1=ALU.subtract).then_inc(lo_ready, 1)
                for i, (rows, _) in enumerate(biases):
                    dve.wait_ge(bias_hi, i + 1)
                    low = rows[BIAS_LO:BIAS_P, :]
                    dve.scalar_tensor_tensor(out=low, in0=bias_stage[BIAS_LO:BIAS_P, i, :], scalar=WS, in1=low,
                                             op0=ALU.mult, op1=ALU.subtract).then_inc(lo_ready, 1)
                dve.wait_ge(lo_ready, len(jobs) + len(biases))


def square_jobs(pair, dram, cols=D):
    view = dram.rearrange("(k p) n -> p k n", p=P)
    step = max(1, 2048 // cols)
    kc = view.shape[1]
    return [(pair[0][:, k:k + step, :], pair[1][:, k:k + step, :], view[:, k:k + step, :])
            for k in range(0, kc, step)]



NORM_BANKS = (6, 7)


class Norm:

    def __init__(self, nc, sb, sem, tag, consts, psum, width=S, first=0, scale=1.0, ahead=False):
        self.ring = sb(f"{tag}_ring", [P, RING, D], F32) if ahead else None
        self.ring_loaded = [sem(f"{tag}_ring_loaded{t}") for t in range(RING)] if ahead else []
        self.x = sb(f"{tag}_x", [P, NT, D], F32)
        self.stats, self.mv = sb(f"{tag}_stats", [P, NT, 6], F32), sb(f"{tag}_mv", [P, NT, 2], F32)
        self.pool_fence = sb(f"{tag}_pool_fence", [P, NT], F32)
        self.rstd, self.fence = sb(f"{tag}_rstd", [P, NT], F32), sb(f"{tag}_fence", [P, 1], F32)
        self.xn = sb(f"{tag}_xn", [P, 2, D], F32)
        self.xt = [sb(f"{tag}_xt{p}", [P, KC, width], F16) for p in range(2)]
        self.first, self.scale, self.consts, self.psum = first, scale, consts, psum
        self.x_loaded, self.stored, self.turn = consts.x_loaded, consts.stored, consts.turn * B
        self.moments, self.eps_added = sem(f"{tag}_moments"), sem(f"{tag}_eps_added")
        self.rstd_ready, self.xn_ready = sem(f"{tag}_rstd_ready"), sem(f"{tag}_xn_ready")
        self.xn_transposed = sem(f"{tag}_xn_transposed")
        self.xt_hi, self.xt_lo = sem(f"{tag}_xt_hi"), sem(f"{tag}_xt_lo")
        self.res_ready = sem(f"{tag}_res_ready")

    def residual_rows(self, engine, b, t):
        if self.ring is None:
            return self.x[:, t, :]
        engine.wait_ge(self.ring_loaded[t % RING], 16 * (NT // RING) * b + 16 * (t // RING + 1))
        return self.ring[:, t % RING, :]


def norm_gpsimd(pool, n, b):
    pool.wait_ge(n.moments, 2 * NT * (b + 1))
    pool.tensor_tensor(n.rstd[:, :], n.mv[:, :, 1], n.consts.eps[:, :], ALU.add).then_inc(n.eps_added, 1)
    pool.wait_ge(n.eps_added, b + 1)
    pool.tensor_tensor(n.rstd[:, :], n.rstd[:, :], n.consts.minus_half[:, :], ALU.pow).then_inc(n.rstd_ready, 1)


def norm_stats(dve, n, b, t):
    dve.wait_ge(n.x_loaded[t], 16 * b + 16 * (n.turn + 1))
    dve.bn_stats(n.stats[:, t, :], n.x[:, t, :]).then_inc(n.moments, 1)


def norm_aggregate(dve, n, b):
    dve.wait_ge(n.moments, 2 * NT * b + NT)
    dve.memset(n.fence[:, :], 0.0)
    for t in range(NT):
        dve.bn_aggr(n.mv[:, t, :], n.stats[:, t, :]).then_inc(n.moments, 1)


def norm_moments(dve, n, b):
    for t in range(NT):
        norm_stats(dve, n, b, t)
    norm_aggregate(dve, n, b)
    dve.wait_ge(n.rstd_ready, b + 1)


def norm_rows(dve, n, b, t):
    if t >= 2:
        dve.wait_ge(n.xn_transposed, NT * b + t - 1)
    dve.tensor_scalar(n.xn[:, t % 2, :], n.x[:, t, :], n.mv[:, t, 0:1], n.rstd[:, t:t + 1],
                      ALU.subtract, ALU.mult).then_inc(n.xn_ready, 1)


def norm_rows_gpsimd(pool, n, b):
    pool.wait_ge(n.rstd_ready, b + 1)
    for t in range(NT):
        if t >= 2:
            pool.wait_ge(n.xn_transposed, NT * b + t - 1)
        pool.tensor_tensor(n.pool_fence[:, t:t + 1], n.consts.eps[:, 0:1], n.consts.eps[:, 0:1], ALU.add)
        pool.tensor_scalar(n.xn[:, t % 2, :], n.x[:, t, :], n.mv[:, t, 0:1], n.rstd[:, t:t + 1],
                           ALU.subtract, ALU.mult).then_inc(n.xn_ready, 1)


def norm_place(n, t, bank):
    return n.psum[:, bank, :].rearrange("p (k c) -> p k c", c=P), slice(n.first + t * P, n.first + (t + 1) * P)


def norm_flip(pe, n, b, t, bank):
    for k in range(KC):
        last = pe.transpose(n.psum[:, bank, k * P:(k + 1) * P], n.xn[:, t % 2, k * P:(k + 1) * P],
                            n.consts.ident[:, :])
    last.then_inc(n.xn_transposed, 1)


def norm_high(act, n, b, t, bank):
    source, cols = norm_place(n, t, bank)
    act.wait_ge(n.xn_transposed, NT * b + t + 1)
    act.activation(n.xt[0][:, :, cols], source, ACT.Copy, scale=n.scale).then_inc(n.xt_hi, 1)


def norm_low(dve, n, b, t, bank):
    source, cols = norm_place(n, t, bank)
    dve.wait_ge(n.xt_hi, NT * b + t + 1)
    dve.scalar_tensor_tensor(out=n.xt[1][:, :, cols], in0=source, scalar=n.scale, in1=n.xt[0][:, :, cols],
                             op0=ALU.mult, op1=ALU.subtract).then_inc(n.xt_lo, 1)


def norm_vector(dve, n, b):
    norm_moments(dve, n, b)
    norm_rows(dve, n, b, 0)
    for t in range(NT):
        if t + 1 < NT:
            norm_rows(dve, n, b, t + 1)
        norm_low(dve, n, b, t, NORM_BANKS[t % 2])


def norm_tensor(pe, n, b):
    for t in range(NT):
        pe.wait_ge(n.xn_ready, NT * b + t + 1)
        if t >= 2:
            pe.wait_ge(n.xt_lo, NT * b + t - 1)
        norm_flip(pe, n, b, t, NORM_BANKS[t % 2])


def norm_scalar(act, n, b):
    for t in range(NT):
        norm_high(act, n, b, t, NORM_BANKS[t % 2])


def stream_rows(sp, n, x_in, x_out, between=None):
    def load(b, t):
        sp.dma_start(n.x[:, t, :], tokens_in(x_in, b, t)).then_inc(n.x_loaded[t], 16)

    def store(b, t):
        sp.wait_ge(n.res_ready, NT * b + t + 1)
        sp.dma_start(tokens_in(x_out, b, t), n.x[:, t, :]).then_inc(n.stored[t], 16)

    for t in range(NT):
        load(0, t)
    with sp.Fori(0, B - 1) as b:
        if between is not None:
            between(b)
        for t in range(NT + 1):
            if t < NT:
                store(b, t)
            if t >= 1:
                sp.wait_ge(n.stored[t - 1], 16 * b + 16 * (n.turn + 1))
                load(b + 1, t - 1)
    for t in range(NT):
        store(B - 1, t)
    for t in range(NT):
        sp.wait_ge(n.stored[t], 16 * (n.turn + B))



RING = 4


def sequences(engine, body):
    with engine.Fori(0, B - 1) as b:
        body(b, True)
    body(B - 1, False)


def stream_ahead(sp, n, x_in, x_out, between=None):
    def load(b, t):
        sp.dma_start(n.x[:, t % NT, :], tokens_in(x_in, b, t)).then_inc(n.x_loaded[t % NT], 16)

    def load_again(b, t):
        sp.dma_start(n.ring[:, t % RING, :], tokens_in(x_in, b, t)).then_inc(n.ring_loaded[t % RING], 16)

    def store(b, t):
        sp.wait_ge(n.res_ready, NT * b + t + 1)
        sp.dma_start(tokens_in(x_out, b, t), n.ring[:, t % RING, :]).then_inc(n.stored[t], 16)

    def stored(b, t):
        sp.wait_ge(n.stored[t], 16 * b + 16 * (n.turn + 1))

    def sequence(b, follows):
        if follows:
            sp.wait_ge(n.xn_ready, NT * (b + 1))
            for t in range(NT):
                load(b, NT + t)
            if between is not None:
                between(b)
        for t in range(NT + 1):
            if t < NT:
                store(b, t)
            if t >= 1 and (t <= RING or follows):
                stored(b, t - 1)
                load_again(b, t - 1 + RING)
        if not follows:
            for t in range(RING, NT):
                stored(b, t)

    for t in range(NT):
        load(0, t)
    for t in range(RING):
        load_again(0, t)
    sequences(sp, sequence)


class OutProjection:

    def __init__(self, ot, wo, bias, projected):
        self.ot, self.wo, self.bias, self.projected = ot, wo, bias, projected


def out_projection_tensor(pe, n, o, b):
    chunks = o.wo[0].shape[1]
    for t in range(NT):
        if t >= 4:
            pe.wait_ge(n.res_ready, NT * b + t - 3)
        for i, (k, (p, q)) in enumerate((k, term) for k in range(chunks) for term in TERMS):
            last = pe.matmul(n.psum[:, t % 4, :], o.ot[p][:, k, t * P:(t + 1) * P], o.wo[q][:, k, :],
                             start=(i == 0), stop=(i == 3 * chunks - 1 and o.bias is None))
        if o.bias is not None:
            last = pe.matmul(n.psum[:, t % 4, :], n.consts.ones[:, 0:P], o.bias, start=False, stop=True)
        last.then_inc(o.projected, 1)


def out_projection_vector(dve, n, o, b):
    for t in range(NT):
        rows = n.residual_rows(dve, b, t)
        dve.wait_ge(o.projected, NT * b + t + 1)
        dve.scalar_tensor_tensor(out=rows, in0=n.psum[:, t % 4, :], scalar=1 / WS, in1=rows,
                                 op0=ALU.mult, op1=ALU.add).then_inc(n.res_ready, 1)



H = 16
DH = D // H
GR = P // DH
VC = DH + 1
FLIP_BANKS = (4, 5)


class LocalHeads:

    def __init__(self, nc, sb, sem, tag, consts, psum, tiles, rows, blocks, mask, qt, kt, v, ot):
        self.consts, self.psum, self.mask = consts, psum, mask
        self.qt, self.kt, self.v, self.ot = qt, kt, v, ot
        self.tiles, self.rows, self.blocks = tiles, rows, blocks
        self.chunks = 4 // blocks
        self.heads = 2 * self.chunks
        self.per_tile = H // self.heads
        self.units = tiles * self.per_tile
        self.probs = sb(f"{tag}_probs", [P, 2, 2, self.chunks, blocks * P], F32)
        self.pt = [sb(f"{tag}_pt{p}", [P, 2, 2, 4, P], F16) for p in range(2)]
        self.neg_max = sb(f"{tag}_neg_max", [P, 2, self.heads], F32)
        self.inv_sum = sb(f"{tag}_inv_sum", [P, 2, self.heads], F32)
        self.out = sb(f"{tag}_heads_out", [P, 2, KC, 2, 2, DH], F32)
        self.scored, self.maxed, self.exped = (sem(f"{tag}_{s}") for s in ("scored", "maxed", "exped"))
        self.flipped, self.flip_hi, self.flip_lo = (sem(f"{tag}_{s}") for s in ("flipped", "flip_hi", "flip_lo"))
        self.weighted, self.summed, self.normed = (sem(f"{tag}_{s}") for s in ("weighted", "summed", "normed"))
        self.order = [g for step in range(self.units + 2) for g in self.groups(step)]
        self.place = {g: i for i, g in enumerate(self.order)}

    def unit(self, u):
        tile, at = divmod(u, self.per_tile)
        return tile, (at // 2) * self.chunks, at % 2

    def first_key(self, u):
        return P if self.blocks == 2 and u < self.per_tile else 0

    def unit_groups(self, u):
        return [("probs", u, i) for i in range(2) if not (self.first_key(u) and i == 0)]

    def groups(self, step):
        mine = self.unit_groups(step) if step < self.units else []
        done = step - 2
        out = [("out", done // self.per_tile, 0)] if done >= 0 and done % self.per_tile == self.per_tile - 1 else []
        return mine + out

    def first_exps(self, u, i):
        return self.heads if self.blocks == 2 else 4 * (i + 1)

    def bank(self, group):
        f = self.place[group]
        return self.psum[:, FLIP_BANKS[f % 2], :].rearrange("p (h q) -> p h q", q=P)[:, :, 0:self.rows]

    def destination(self, group):
        kind, index, i = group
        if kind == "probs":
            return [self.pt[p][:, index % 2, i, :, 0:self.rows] for p in range(2)]
        return [self.ot[p][:, :, index * self.rows:(index + 1) * self.rows] for p in range(2)]

    def scores(self, u):
        return self.psum[:, 2 * (u % 2):2 * (u % 2) + 2, :]\
            .rearrange("p j (g c) -> p (j g) c", c=self.blocks * P)[:, :, self.first_key(u):]


    def score(self, pe, u):
        tile, g0, s = self.unit(u)
        k0, width = self.first_key(u), self.blocks * P
        queries = slice(tile * self.rows, tile * self.rows + P)
        first = (tile - 1) * P + k0 if self.blocks == 2 else tile * self.rows
        keys = slice(first, first + width - k0)
        for g in range(self.chunks):
            for i, (p, q) in enumerate(TERMS):
                for j in range(2):
                    r = slice(DH * (2 * s + j), DH * (2 * s + j + 1))
                    last = pe.matmul(self.psum[:, 2 * (u % 2) + j, g * width + k0:(g + 1) * width],
                                     self.qt[p][r, g0 + g, queries], self.kt[q][r, g0 + g, keys],
                                     start=(i == 0), stop=(i == 2))
                if i == 0:
                    for j in range(2):
                        pe.matmul(self.psum[:, 2 * (u % 2) + j, (g + 1) * width - P:(g + 1) * width],
                                  self.consts.ident_b[:, :], self.mask[:, :], start=False, stop=False)
        last.then_inc(self.scored, 1)

    def flip(self, pe, b, group):
        kind, index, i = group
        f = self.place[group]
        bank = self.psum[:, FLIP_BANKS[f % 2], :]
        if f >= 2:
            pe.wait_ge(self.flip_lo, len(self.order) * b + f - 1)
        if kind == "probs":
            pe.wait_ge(self.exped, self.heads * (self.units * b + index) + self.first_exps(index, i))
            for slot in range(4):
                g, j = slot // 2, slot % 2
                if self.blocks == 2:
                    source = self.probs[:, index % 2, j, g, i * P:(i + 1) * P]
                else:
                    source = self.probs[:, index % 2, j, 2 * i + g, :]
                last = pe.transpose(bank[:, slot * P:(slot + 1) * P], source, self.consts.ident[:, :])
        else:
            pe.wait_ge(self.normed, self.units * b + (index + 1) * self.per_tile)
            for k in range(KC):
                last = pe.transpose(bank[:, k * P:(k + 1) * P],
                                    self.out[:, index % 2, k, :, :, :].rearrange("p a j d -> p (a j d)"),
                                    self.consts.ident[:, :])
        last.then_inc(self.flipped, 1)

    def weigh(self, pe, b, u):
        tile, g0, s = self.unit(u)
        for group in self.unit_groups(u):
            pe.wait_ge(self.flip_lo, len(self.order) * b + self.place[group] + 1)
        if u >= 2:
            pe.wait_ge(self.normed, self.units * b + u - 1)
        for g in range(self.chunks):
            for j in range(2):
                head, at = GR * (g0 + g) + 2 * s + j, g * 2 + j
                if self.blocks == 2:
                    parts = [(i, at, tile - 1 + i) for i in range(self.first_key(u) // P, 2)]
                else:
                    parts = [(at // 4, at % 4, tile)]
                terms = [(*part, p, q) for part in parts for p, q in TERMS]
                for n, (i, slot, block, p, q) in enumerate(terms):
                    last = pe.matmul(self.psum[:, 6 + u % 2, at * VC:(at + 1) * VC],
                                     self.pt[p][:, u % 2, i, slot, :], self.v[q][:, block, head, :],
                                     start=(n == 0), stop=(n == len(terms) - 1))
        last.then_inc(self.weighted, 1)

    def tensor(self, pe, b):
        self.score(pe, 0)
        for step in range(self.units + 2):
            if step + 1 < self.units:
                self.score(pe, step + 1)
            for group in self.groups(step):
                self.flip(pe, b, group)
            if 1 <= step <= self.units:
                self.weigh(pe, b, step - 1)
        pe.wait_ge(self.flip_lo, len(self.order) * (b + 1))


    def exponentials(self, act, b, u):
        act.wait_ge(self.maxed, self.units * b + u + 1)
        k0, width = self.first_key(u), self.blocks * P
        for g in range(self.chunks):
            for j in range(2):
                h = self.chunks * j + g
                act.activation(self.probs[:, u % 2, j, g, k0:],
                               self.psum[:, 2 * (u % 2) + j, g * width + k0:(g + 1) * width], ACT.Exp,
                               bias=self.neg_max[:, u % 2, h:h + 1]).then_inc(self.exped, 1)

    def scalar(self, act, b):
        self.exponentials(act, b, 0)
        for step in range(self.units + 2):
            for group in self.groups(step):
                act.wait_ge(self.flipped, len(self.order) * b + self.place[group] + 1)
                act.activation(self.destination(group)[0], self.bank(group), ACT.Copy).then_inc(self.flip_hi, 1)
            if step + 1 < self.units:
                self.exponentials(act, b, step + 1)


    def maxima(self, dve, b, u):
        dve.wait_ge(self.scored, self.units * b + u + 1)
        dve.tensor_reduce(out=self.neg_max[:, u % 2, :], in_=self.scores(u), axis=X_AXIS, op=ALU.max,
                          negate=True).then_inc(self.maxed, 1)

    def normalize(self, dve, b, u):
        tile, g0, s = self.unit(u)
        got = self.psum[:, 6 + u % 2, 0:self.heads * VC].rearrange("p (g j c) -> p g j c", j=2, c=VC)
        inv = self.inv_sum[:, u % 2, :].rearrange("p (g j) -> p g j", j=2)
        dve.wait_ge(self.weighted, self.units * b + u + 1)
        dve.reciprocal(inv, got[:, :, :, DH]).then_inc(self.summed, 1)
        dve.wait_ge(self.summed, self.units * b + u + 1)
        dve.tensor_tensor(self.out[:, tile % 2, g0:g0 + self.chunks, s, :, :], got[:, :, :, 0:DH],
                          inv.unsqueeze(3).to_broadcast([P, self.chunks, 2, DH]), ALU.mult).then_inc(self.normed, 1)

    def vector(self, dve, b):
        self.maxima(dve, b, 0)
        for step in range(self.units + 2):
            if step + 1 < self.units:
                self.maxima(dve, b, step + 1)
            for group in self.groups(step):
                hi, lo = self.destination(group)
                dve.wait_ge(self.flip_hi, len(self.order) * b + self.place[group] + 1)
                dve.tensor_tensor(lo, self.bank(group), hi, ALU.subtract).then_inc(self.flip_lo, 1)
            if 1 <= step <= self.units:
                self.normalize(dve, b, step - 1)



HALF_WIN = 16
QW = P - 2 * HALF_WIN
NW = -(-S // QW)
PADDED = QW * (NW - 1) + P
SQ = PADDED


def window_attention(nc, consts, psum, x_in, x_out, dram):
    stack, sb, sem = scoped(nc)
    with stack:
        wq, wk, wv, wo = ([sb(f"wa_w{m}{p}", [P, KC, D], F16) for p in range(2)] for m in "qkvo")
        bias = {m: sb(f"wa_b{m}", [BIAS_P, D], F16) for m in "qkvo"}
        split_weights(nc, "wa", [j for pair, matrix in ((wq, dram["l0_wq"]), (wk, dram["l0_wk"]), (wv, dram["l0_wv"]), (wo, dram["l0_wo"]))
                                 for j in square_jobs(pair, matrix)],
                      [(bias["q"][:, :], dram["l0_bq"]), (bias["k"][:, :], dram["l0_bk"]), (bias["v"][:, :], dram["l0_bv"]), (bias["o"][:, :], dram["l0_bo"])])

        n = Norm(nc, sb, sem, "wa", consts, psum, width=PADDED, first=HALF_WIN)
        valid = sb("wa_valid", [BIAS_P, PADDED], F16)
        mask = sb("wa_mask", [P, P], BF16)
        qt = [sb(f"wa_qt{p}", [P, KC, SQ], F16) for p in range(2)]
        kt = [sb(f"wa_kt{p}", [P, KC, PADDED], F16) for p in range(2)]
        v = [sb(f"wa_v{p}", [P, NW, H, VC], F16) for p in range(2)]
        ot = [sb(f"wa_ot{p}", [P, KC, SQ], F16) for p in range(2)]
        ready = sem("wa_ready")
        mask_filled = sem("wa_mask_filled")
        projected, proj_hi, proj_lo = sem("wa_projected"), sem("wa_proj_hi"), sem("wa_proj_lo")
        local = LocalHeads(nc, sb, sem, "wa", consts, psum, NW, QW, 1, mask, qt, kt, v, ot)
        o = OutProjection(ot=ot, wo=wo, bias=bias["o"][:, :], projected=sem("wa_out_projected"))

        qscale = 1.0 / (WS * DH ** 0.5)
        QK_ITEMS = 2 * KC * 2
        ITEMS = QK_ITEMS + NW
        real_cols = slice(HALF_WIN, HALF_WIN + S)

        def item(i):
            if i < QK_ITEMS:
                m, half = (i % (2 * KC)) // 2, i % 2
                first = half * 512 + (HALF_WIN if i >= QK_ITEMS // 2 else 0)
                out = qt if i < QK_ITEMS // 2 else kt
                return [out[p][:, m, first:first + 512] for p in range(2)], \
                    psum[:, i % 4, :], (qscale if i < QK_ITEMS // 2 else 1 / WS)
            return [v[p][:, i - QK_ITEMS, :, 0:DH] for p in range(2)], \
                psum[:, i % 4, :].rearrange("p (h d) -> p h d", d=DH), 1 / WS

        with nc.Block() as block:
            @block.sync
            def _(sp):
                stream_rows(sp, n, x_in, x_out)

            @block.gpsimd
            def _(pool):
                for part in range(2):
                    for edge in (slice(0, HALF_WIN), slice(HALF_WIN + S, PADDED)):
                        pool.memset(n.xt[part][:, :, edge], 0.0)
                        pool.memset(kt[part][:, :, edge], 0.0)
                    pool.memset(qt[part][:, :, S:SQ], 0.0)
                    pool.memset(local.pt[part][:, :, :, :, QW:P], 1.0)
                pool.memset(v[0][:, :, :, :], 1.0)
                pool.memset(v[1][:, :, :, :], 0.0)
                pool.memset(valid[:, :], 0.0).then_inc(mask_filled, 1)
                pool.memset(mask[:, :], 0.0).then_inc(mask_filled, 1)
                pool.wait_ge(mask_filled, 2)
                pool.memset(valid[:, real_cols], 1.0)
                pool.affine_select(out=mask[:, :], in_=mask[:, :], compare_op=ALU.is_ge, fill=MASKED, base=0,
                                   pattern=[[1, P]], channel_multiplier=-1).then_inc(mask_filled, 1)
                pool.wait_ge(mask_filled, 3)
                pool.affine_select(out=mask[:, :], in_=mask[:, :], compare_op=ALU.is_ge, fill=MASKED,
                                   base=2 * HALF_WIN, pattern=[[-1, P]], channel_multiplier=1).then_inc(ready, 1)
                with pool.Fori(0, B) as b:
                    norm_gpsimd(pool, n, b)

            @block.tensor
            def _(pe):
                pe.wait_ge(ready, 1)

                def project(b, i):
                    if i >= 4:
                        pe.wait_ge(proj_lo, ITEMS * b + i - 3)
                    bank = psum[:, i % 4, :]
                    if i < QK_ITEMS:
                        m, half = (i % (2 * KC)) // 2, i % 2
                        wt, bw = (wq, bias["q"]) if i < QK_ITEMS // 2 else (wk, bias["k"])
                        cols = slice(HALF_WIN + half * 512, HALF_WIN + half * 512 + 512)
                        for k in range(KC):
                            for p, q in TERMS:
                                pe.matmul(bank, wt[p][:, k, m * P:(m + 1) * P], n.xt[q][:, k, cols],
                                          start=(k == 0 and (p, q) == (0, 0)), stop=False)
                        pe.matmul(bank, bw[:, m * P:(m + 1) * P], consts.ones[:, 0:512],
                                  start=False, stop=True).then_inc(projected, 1)
                    else:
                        win = i - QK_ITEMS
                        cols = slice(win * QW, win * QW + P)
                        for k in range(KC):
                            for p, q in TERMS:
                                pe.matmul(bank, n.xt[p][:, k, cols], wv[q][:, k, :],
                                          start=(k == 0 and (p, q) == (0, 0)), stop=False)
                        pe.matmul(bank, valid[:, cols], bias["v"][:, :],
                                  start=False, stop=True).then_inc(projected, 1)

                with pe.Fori(0, B) as b:
                    norm_tensor(pe, n, b)
                    pe.wait_ge(n.xt_lo, NT * (b + 1))
                    for i in range(ITEMS):
                        project(b, i)
                    pe.wait_ge(proj_lo, ITEMS * (b + 1))
                    local.tensor(pe, b)
                    out_projection_tensor(pe, n, o, b)

            @block.scalar
            def _(act):
                with act.Fori(0, B) as b:
                    norm_scalar(act, n, b)
                    for i in range(ITEMS):
                        out, bank, scale = item(i)
                        act.wait_ge(projected, ITEMS * b + i + 1)
                        act.activation(out[0], bank, ACT.Copy, scale=scale).then_inc(proj_hi, 1)
                    local.scalar(act, b)

            @block.vector
            def _(dve):
                with dve.Fori(0, B) as b:
                    norm_vector(dve, n, b)
                    for i in range(ITEMS):
                        out, bank, scale = item(i)
                        dve.wait_ge(proj_hi, ITEMS * b + i + 1)
                        dve.scalar_tensor_tensor(out=out[1], in0=bank, scalar=scale, in1=out[0],
                                                 op0=ALU.mult, op1=ALU.subtract).then_inc(proj_lo, 1)
                    local.vector(dve, b)
                    out_projection_vector(dve, n, o, b)



def block_attention(nc, consts, psum, x_in, x_out, dram):
    stack, sb, sem = scoped(nc)
    with stack:
        wo = [sb(f"ba_wo{p}", [P, KC, D], F16) for p in range(2)]
        bias = sb("ba_bo", [BIAS_P, D], F16)
        split_weights(nc, "ba", square_jobs(wo, dram["l0_xo"]), [(bias[:, :], dram["l0_xbo"])])

        n = Norm(nc, sb, sem, "ba", consts, psum, scale=DH ** -0.5)
        qt = n.xt
        mask = sb("ba_mask", [P, P], BF16)
        kt_stage, v_stage = sb("ba_kt_stage", [P, KC, S], F32), sb("ba_v_stage", [P, NT, D], F32)
        kt = [sb(f"ba_kt{p}", [P, KC, S], F16) for p in range(2)]
        v = [sb(f"ba_v{p}", [P, NT, H, VC], F16) for p in range(2)]
        ot = [sb(f"ba_ot{p}", [P, KC, S], F16) for p in range(2)]
        ready, mask_filled = sem("ba_ready"), sem("ba_mask_filled")
        ctx_loaded, ctx_hi, ctx_lo = sem("ba_ctx_loaded"), sem("ba_ctx_hi"), sem("ba_ctx_lo")
        kept = sem("ba_kept")
        local = LocalHeads(nc, sb, sem, "ba", consts, psum, NT, P, 2, mask, qt, kt, v, ot)
        o = OutProjection(ot=ot, wo=wo, bias=bias[:, :], projected=sem("ba_out_projected"))

        splits = [(kt[0][:, k, :], kt[1][:, k, :], kt_stage[:, k, :]) for k in range(KC)] + \
            [(v[0][:, t, :, 0:DH], v[1][:, t, :, 0:DH],
              v_stage[:, t, :].rearrange("p (h d) -> p h d", d=DH)) for t in range(NT)]

        with nc.Block() as block:
            @block.sync
            def _(sp):
                def load_context(b):
                    sp.dma_start(kt_stage[:, :, :], dram["ctx_t"][bass.ds(b * D, D), :]
                                 .rearrange("(k p) s -> p k s", p=P)).then_inc(ctx_loaded, 16)
                    sp.dma_start(v_stage[:, :, :], dram["ctx"][bass.ds(b * S, S), :]
                                 .rearrange("(t p) d -> p t d", p=P)).then_inc(ctx_loaded, 16)

                def keep_context(b):
                    sp.wait_ge(ctx_lo, len(splits) * (b + 1))
                    for p in range(2):
                        sp.dma_start(dram["ctx_parts"][p][bass.ds(b * P, P), :],
                                     kt[p][:, :, :].rearrange("p k s -> p (k s)")).then_inc(kept, 16)
                    sp.wait_ge(kept, 32 * (b + 1))

                def between(b):
                    keep_context(b)
                    load_context(b + 1)

                load_context(0)
                stream_rows(sp, n, x_in, x_out, between)
                keep_context(B - 1)

            @block.gpsimd
            def _(pool):
                pool.memset(v[0][:, :, :, :], 1.0).then_inc(ready, 1)
                pool.memset(v[1][:, :, :, :], 0.0).then_inc(ready, 1)
                pool.memset(mask[:, :], 0.0).then_inc(mask_filled, 1)
                pool.wait_ge(mask_filled, 1)
                pool.affine_select(out=mask[:, :], in_=mask[:, :], compare_op=ALU.is_ge, fill=MASKED, base=0,
                                   pattern=[[-1, P]], channel_multiplier=1).then_inc(ready, 1)
                with pool.Fori(0, B) as b:
                    norm_gpsimd(pool, n, b)

            @block.tensor
            def _(pe):
                pe.wait_ge(ready, 3)

                with pe.Fori(0, B) as b:
                    norm_tensor(pe, n, b)
                    pe.wait_ge(n.xt_lo, NT * (b + 1))
                    pe.wait_ge(ctx_lo, len(splits) * (b + 1))
                    local.tensor(pe, b)
                    out_projection_tensor(pe, n, o, b)

            @block.scalar
            def _(act):
                act.wait_ge(ready, 3)
                with act.Fori(0, B) as b:
                    act.wait_ge(ctx_loaded, 32 * (b + 1))
                    for hi, _, full in splits:
                        act.activation(hi, full, ACT.Copy).then_inc(ctx_hi, 1)
                    norm_scalar(act, n, b)
                    local.scalar(act, b)

            @block.vector
            def _(dve):
                with dve.Fori(0, B) as b:
                    for i, (hi, lo, full) in enumerate(splits):
                        dve.wait_ge(ctx_hi, len(splits) * b + i + 1)
                        dve.tensor_tensor(lo, full, hi, ALU.subtract).then_inc(ctx_lo, 1)
                    norm_vector(dve, n, b)
                    local.vector(dve, b)
                    out_projection_vector(dve, n, o, b)



E = 8
R = 16
TOP_K = 2


def expert_ffn(nc, consts, psum, x_in, x_out, dram):
    stack, sb, sem = scoped(nc)
    with stack:
        GA = E + E * R
        wga = [sb(f"ef_wga{p}", [P, KC, GA], F16) for p in range(2)]
        wb = [sb(f"ef_wb{p}", [P, 1, D], F16) for p in range(2)]
        view = lambda a: a.rearrange("(k p) n -> p k n", p=P)
        split_weights(nc, "ef", [
            (wga[0][:, :, 0:E], wga[1][:, :, 0:E], view(dram["l0_g"])),
            (wga[0][:, :, E:GA], wga[1][:, :, E:GA], view(dram["l0_a"])),
            (wb[0][:, :, :], wb[1][:, :, :], view(dram["l0_b"]))])

        n = Norm(nc, sb, sem, "ef", consts, psum)
        gh = sb("ef_gh", [P, NT, GA], F32)
        logits, hidden = gh[:, :, 0:E], gh[:, :, E:GA].rearrange("p t (e r) -> p t e r", r=R)
        before = sb("ef_before", [P, E, E], F32)
        larger, equal = sb("ef_larger", [P, NT, E, E], F32), sb("ef_equal", [P, NT, E, E], F32)
        rank, chosen = sb("ef_rank", [P, NT, E], F32), sb("ef_chosen", [P, NT, E], F32)
        top, total = sb("ef_top", [P, NT], F32), sb("ef_total", [P, NT], F32)
        share = sb("ef_share", [P, NT, E], F32)
        hw = sb("ef_hw", [P, NT, E, R], F32)
        hwt = [sb(f"ef_hwt{p}", [P, 1, S], F16) for p in range(2)]
        before_filled = sem("ef_before_filled")
        projected, gathered = sem("ef_projected"), sem("ef_gathered")
        gate_step, shifted, exped = sem("ef_gate_step"), sem("ef_shifted"), sem("ef_exped")
        weighed = sem("ef_weighed")
        flipped, flip_hi, flip_lo = sem("ef_flipped"), sem("ef_flip_hi"), sem("ef_flip_lo")
        o = OutProjection(ot=hwt, wo=wb, bias=None, projected=sem("ef_out_projected"))
        FLIPS, GATE_STEPS = 2, 11
        per_expert = [P, NT, E]

        with nc.Block() as block:
            @block.sync
            def _(sp):
                stream_rows(sp, n, x_in, x_out)

            @block.gpsimd
            def _(pool):
                pool.memset(before[:, :, :], 1.0).then_inc(before_filled, 1)
                pool.wait_ge(before_filled, 1)
                pool.affine_select(out=before[:, :, :], in_=before[:, :, :], compare_op=ALU.is_gt, fill=0.0, base=0,
                                   pattern=[[1, E], [-1, E]], channel_multiplier=0).then_inc(before_filled, 1)
                with pool.Fori(0, B) as b:
                    norm_gpsimd(pool, n, b)

            @block.tensor
            def _(pe):
                with pe.Fori(0, B) as b:
                    norm_tensor(pe, n, b)
                    for t in range(NT):
                        pe.wait_ge(n.xt_lo, NT * b + t + 1)
                        if t >= 4:
                            pe.wait_ge(gathered, NT * b + t - 3)
                        for i, (k, (p, q)) in enumerate((k, term) for k in range(KC) for term in TERMS):
                            last = pe.matmul(psum[:, t % 4, 0:GA], n.xt[p][:, k, t * P:(t + 1) * P],
                                             wga[q][:, k, :], start=(i == 0), stop=(i == 3 * KC - 1))
                        last.then_inc(projected, 1)
                    pe.wait_ge(weighed, b + 1)
                    for f in range(FLIPS):
                        for i in range(4):
                            last = pe.transpose(psum[:, 4 + f, i * P:(i + 1) * P],
                                                hw[:, 4 * f + i, :, :].rearrange("p e r -> p (e r)"),
                                                consts.ident[:, :])
                        last.then_inc(flipped, 1)
                    pe.wait_ge(flip_lo, FLIPS * (b + 1))
                    out_projection_tensor(pe, n, o, b)

            @block.scalar
            def _(act):
                with act.Fori(0, B) as b:
                    norm_scalar(act, n, b)
                    for t in range(NT):
                        act.wait_ge(projected, NT * b + t + 1)
                        act.activation(gh[:, t, :], psum[:, t % 4, 0:GA], ACT.Copy, scale=1 / WS).then_inc(gathered, 1)
                    act.wait_ge(shifted, b + 1)
                    act.activation(share[:, :, :], share[:, :, :], ACT.Exp).then_inc(exped, 1)
                    for f in range(FLIPS):
                        act.wait_ge(flipped, FLIPS * b + f + 1)
                        act.activation(hwt[0][:, 0, f * 512:(f + 1) * 512], psum[:, 4 + f, :],
                                       ACT.Copy).then_inc(flip_hi, 1)

            @block.vector
            def _(dve):
                dve.wait_ge(before_filled, 2)
                with dve.Fori(0, B) as b:
                    norm_vector(dve, n, b)
                    done = lambda k: GATE_STEPS * b + k
                    dve.wait_ge(gathered, NT * (b + 1))
                    dve.tensor_reduce(out=top[:, :], in_=logits, axis=X_AXIS, op=ALU.max).then_inc(gate_step, 1)
                    dve.tensor_tensor(larger[:, :, :, :], logits.unsqueeze(2).to_broadcast([P, NT, E, E]),
                                      logits.unsqueeze(3).to_broadcast([P, NT, E, E]), ALU.is_gt).then_inc(gate_step, 1)
                    dve.tensor_tensor(equal[:, :, :, :], logits.unsqueeze(2).to_broadcast([P, NT, E, E]),
                                      logits.unsqueeze(3).to_broadcast([P, NT, E, E]),
                                      ALU.is_equal).then_inc(gate_step, 1)
                    dve.wait_ge(gate_step, done(1))
                    dve.tensor_tensor(share[:, :, :], logits, top[:, :].unsqueeze(2).to_broadcast(per_expert),
                                      ALU.subtract).then_inc(shifted, 1)
                    dve.wait_ge(gate_step, done(3))
                    dve.tensor_tensor(equal[:, :, :, :], equal[:, :, :, :],
                                      before[:, :, :].unsqueeze(1).to_broadcast([P, NT, E, E]),
                                      ALU.mult).then_inc(gate_step, 1)
                    dve.wait_ge(gate_step, done(4))
                    dve.tensor_tensor(larger[:, :, :, :], larger[:, :, :, :], equal[:, :, :, :],
                                      ALU.add).then_inc(gate_step, 1)
                    dve.wait_ge(gate_step, done(5))
                    dve.tensor_reduce(out=rank[:, :, :], in_=larger[:, :, :, :], axis=X_AXIS,
                                      op=ALU.add).then_inc(gate_step, 1)
                    dve.wait_ge(gate_step, done(6))
                    dve.tensor_scalar(chosen[:, :, :], rank[:, :, :], TOP_K - 0.5, None, ALU.is_lt).then_inc(gate_step, 1)
                    dve.wait_ge(gate_step, done(7))
                    dve.wait_ge(exped, b + 1)
                    dve.tensor_tensor(share[:, :, :], share[:, :, :], chosen[:, :, :], ALU.mult).then_inc(gate_step, 1)
                    dve.wait_ge(gate_step, done(8))
                    dve.tensor_reduce(out=total[:, :], in_=share[:, :, :], axis=X_AXIS, op=ALU.add).then_inc(gate_step, 1)
                    dve.wait_ge(gate_step, done(9))
                    dve.reciprocal(total[:, :], total[:, :]).then_inc(gate_step, 1)
                    dve.wait_ge(gate_step, done(10))
                    dve.tensor_tensor(share[:, :, :], share[:, :, :], total[:, :].unsqueeze(2).to_broadcast(per_expert),
                                      ALU.mult).then_inc(gate_step, 1)
                    dve.wait_ge(gate_step, done(11))
                    dve.tensor_tensor(hw[:, :, :, :], hidden, share[:, :, :].unsqueeze(3).to_broadcast([P, NT, E, R]),
                                      ALU.mult).then_inc(weighed, 1)
                    for f in range(FLIPS):
                        cols = slice(f * 512, (f + 1) * 512)
                        dve.wait_ge(flip_hi, FLIPS * b + f + 1)
                        dve.tensor_tensor(hwt[1][:, 0, cols], psum[:, 4 + f, :], hwt[0][:, 0, cols],
                                          ALU.subtract).then_inc(flip_lo, 1)
                    out_projection_vector(dve, n, o, b)



def band_attention(nc, consts, psum, x_in, x_out, dram):
    stack, sb, sem = scoped(nc)
    with stack:
        wq, wk, wv = ([sb(f"bd_w{m}{p}", [P, KC, D], F16) for p in range(2)] for m in "qkv")
        bias = {m: sb(f"bd_b{m}", [BIAS_P, D], F16) for m in "qk"}
        split_weights(nc, "bd", [j for pair, matrix in ((wq, dram["l1_wq"]), (wk, dram["l1_wk"]), (wv, dram["l1_wv"]))
                                 for j in square_jobs(pair, matrix)],
                      [(bias["q"][:, :], dram["l1_bq"]), (bias["k"][:, :], dram["l1_bk"])])

        n = Norm(nc, sb, sem, "bd", consts, psum)
        v_bias = sb("bd_v_bias", [P, D], F32)
        behind, ahead = sb("bd_behind", [P, P], BF16), sb("bd_ahead", [P, P], BF16)
        qt = [sb(f"bd_qt{p}", [P, KC, S], F16) for p in range(2)]
        kt = [sb(f"bd_kt{p}", [P, KC, S], F16) for p in range(2)]
        v = [sb(f"bd_v{p}", [P, NT, D], F16) for p in range(2)]
        probs = sb("bd_probs", [P, 2, 3, P], F32)
        pt = [sb(f"bd_pt{p}", [P, 2, 3, P], F16) for p in range(2)]
        neg_max, total = sb("bd_neg_max", [P, 2], F32), sb("bd_total", [P, 2], F32)
        ready, mask_filled, biased = sem("bd_ready"), sem("bd_mask_filled"), sem("bd_biased")
        v_bias_loaded = sem("bd_v_bias_loaded")
        projected, proj_hi, proj_lo = sem("bd_projected"), sem("bd_proj_hi"), sem("bd_proj_lo")
        scored, maxed, exped = sem("bd_scored"), sem("bd_maxed"), sem("bd_exped")
        flipped, flip_hi, flip_lo = sem("bd_flipped"), sem("bd_flip_hi"), sem("bd_flip_lo")
        weighted, inverted = sem("bd_weighted"), sem("bd_inverted")
        qscale = 1.0 / (WS * D ** 0.5)
        QK = 4 * KC
        ITEMS = QK + NT

        def item(i):
            if i < QK:
                m, half = (i % (2 * KC)) // 2, i % 2
                out = qt if i < QK // 2 else kt
                return [out[p][:, m, half * 512:(half + 1) * 512] for p in range(2)], \
                    (qscale if i < QK // 2 else 1 / WS)
            return [v[p][:, i - QK, :] for p in range(2)], 1 / WS

        def blocks(t):
            return [kb for kb in (t - 1, t, t + 1) if 0 <= kb < NT]

        with nc.Block() as block:
            @block.sync
            def _(sp):
                sp.dma_start(v_bias[:, :], dram["l1_bv"].to_broadcast([P, D])).then_inc(v_bias_loaded, 16)
                stream_rows(sp, n, x_in, x_out)

            @block.gpsimd
            def _(pool):
                pool.memset(behind[:, :], 0.0).then_inc(mask_filled, 1)
                pool.memset(ahead[:, :], 0.0).then_inc(mask_filled, 1)
                pool.wait_ge(mask_filled, 2)
                pool.affine_select(out=behind[:, :], in_=behind[:, :], compare_op=ALU.is_ge, fill=MASKED, base=0,
                                   pattern=[[1, P]], channel_multiplier=-1).then_inc(ready, 1)
                pool.affine_select(out=ahead[:, :], in_=ahead[:, :], compare_op=ALU.is_ge, fill=MASKED, base=0,
                                   pattern=[[-1, P]], channel_multiplier=1).then_inc(ready, 1)
                pool.wait_ge(v_bias_loaded, 16)
                with pool.Fori(0, B) as b:
                    norm_gpsimd(pool, n, b)
                    for t in range(NT):
                        pool.wait_ge(n.xn_ready, NT * b + t + 1)
                        pool.tensor_tensor(n.x[:, t, :], n.x[:, t, :], v_bias[:, :], ALU.add).then_inc(biased, 1)

            @block.tensor
            def _(pe):
                pe.wait_ge(ready, 2)

                def project(b, i):
                    if i >= 4:
                        pe.wait_ge(proj_lo, ITEMS * b + i - 3)
                    bank = psum[:, i % 4, :]
                    terms = [(k, p, q) for k in range(KC) for p, q in TERMS]
                    if i < QK:
                        m, half = (i % (2 * KC)) // 2, i % 2
                        wt, bw = (wq, bias["q"]) if i < QK // 2 else (wk, bias["k"])
                        cols = slice(half * 512, (half + 1) * 512)
                        for k, p, q in terms:
                            pe.matmul(bank, wt[p][:, k, m * P:(m + 1) * P], n.xt[q][:, k, cols],
                                      start=((k, p, q) == terms[0]), stop=False)
                        pe.matmul(bank, bw[:, m * P:(m + 1) * P], consts.ones[:, 0:512],
                                  start=False, stop=True).then_inc(projected, 1)
                    else:
                        cols = slice((i - QK) * P, (i - QK + 1) * P)
                        for k, p, q in terms:
                            last = pe.matmul(bank, n.xt[p][:, k, cols], wv[q][:, k, :],
                                             start=((k, p, q) == terms[0]), stop=((k, p, q) == terms[-1]))
                        last.then_inc(projected, 1)

                def score(t):
                    kbs = blocks(t)
                    bank = psum[:, t % 2, :]
                    cols = slice(kbs[0] * P, (kbs[-1] + 1) * P)
                    for k in range(KC):
                        for p, q in TERMS:
                            if (k, p, q) == (KC - 1, *TERMS[-1]):
                                for kb, m in ((t - 1, behind), (t + 1, ahead)):
                                    if kb in kbs:
                                        at = kbs.index(kb) * P
                                        pe.matmul(bank[:, at:at + P], consts.ident_b[:, :], m[:, :],
                                                  start=False, stop=False)
                            last = pe.matmul(bank[:, 0:len(kbs) * P], qt[p][:, k, t * P:(t + 1) * P],
                                             kt[q][:, k, cols], start=(k == 0 and (p, q) == (0, 0)),
                                             stop=(k == KC - 1 and (p, q) == TERMS[-1]))
                    last.then_inc(scored, 1)

                def flip(b, t):
                    pe.wait_ge(exped, NT * b + t + 1)
                    for i in range(len(blocks(t))):
                        last = pe.transpose(psum[:, 2 + t % 2, i * P:(i + 1) * P], probs[:, t % 2, i, :],
                                            consts.ident[:, :])
                    last.then_inc(flipped, 1)

                def weigh(b, t):
                    pe.wait_ge(flip_lo, NT * b + t + 1)
                    if t >= 2:
                        pe.wait_ge(n.res_ready, NT * b + t - 1)
                    terms = [(i, kb, p, q) for i, kb in enumerate(blocks(t)) for p, q in TERMS]
                    for i, kb, p, q in terms:
                        last = pe.matmul(psum[:, 4 + t % 2, :], pt[p][:, t % 2, i, :], v[q][:, kb, :],
                                         start=((i, kb, p, q) == terms[0]), stop=((i, kb, p, q) == terms[-1]))
                    last.then_inc(weighted, 1)

                with pe.Fori(0, B) as b:
                    norm_tensor(pe, n, b)
                    pe.wait_ge(n.xt_lo, NT * (b + 1))
                    for i in range(ITEMS):
                        project(b, i)
                    pe.wait_ge(proj_lo, ITEMS * (b + 1))
                    score(0)
                    for t in range(NT):
                        if t + 1 < NT:
                            score(t + 1)
                        flip(b, t)
                        if t >= 1:
                            weigh(b, t - 1)
                    weigh(b, NT - 1)

            @block.scalar
            def _(act):
                with act.Fori(0, B) as b:
                    norm_scalar(act, n, b)
                    for i in range(ITEMS):
                        out, scale = item(i)
                        act.wait_ge(projected, ITEMS * b + i + 1)
                        act.activation(out[0], psum[:, i % 4, :], ACT.Copy, scale=scale).then_inc(proj_hi, 1)
                    for t in range(NT):
                        m = len(blocks(t))
                        act.wait_ge(maxed, NT * b + t + 1)
                        act.activation(probs[:, t % 2, 0:m, :],
                                       psum[:, t % 2, 0:m * P].rearrange("p (i c) -> p i c", c=P), ACT.Exp,
                                       bias=neg_max[:, t % 2:t % 2 + 1],
                                       accum_out=total[:, t % 2:t % 2 + 1]).then_inc(exped, 1)
                        act.wait_ge(flipped, NT * b + t + 1)
                        act.activation(pt[0][:, t % 2, 0:m, :],
                                       psum[:, 2 + t % 2, 0:m * P].rearrange("p (i c) -> p i c", c=P),
                                       ACT.Copy).then_inc(flip_hi, 1)

            @block.vector
            def _(dve):
                def maxima(b, t):
                    dve.wait_ge(scored, NT * b + t + 1)
                    dve.tensor_reduce(out=neg_max[:, t % 2:t % 2 + 1], in_=psum[:, t % 2, 0:len(blocks(t)) * P],
                                      axis=X_AXIS, op=ALU.max, negate=True).then_inc(maxed, 1)

                def residual(b, t):
                    dve.wait_ge(weighted, NT * b + t + 1)
                    dve.wait_ge(biased, NT * b + t + 1)
                    dve.scalar_tensor_tensor(out=n.x[:, t, :], in0=psum[:, 4 + t % 2, :],
                                             scalar=total[:, t % 2:t % 2 + 1], in1=n.x[:, t, :],
                                             op0=ALU.mult, op1=ALU.add).then_inc(n.res_ready, 1)

                with dve.Fori(0, B) as b:
                    norm_vector(dve, n, b)
                    for i in range(ITEMS):
                        out, scale = item(i)
                        dve.wait_ge(proj_hi, ITEMS * b + i + 1)
                        dve.scalar_tensor_tensor(out=out[1], in0=psum[:, i % 4, :], scalar=scale, in1=out[0],
                                                 op0=ALU.mult, op1=ALU.subtract).then_inc(proj_lo, 1)
                    maxima(b, 0)
                    for t in range(NT):
                        m = len(blocks(t))
                        if t >= 1:
                            residual(b, t - 1)
                        if t + 1 < NT:
                            maxima(b, t + 1)
                        dve.wait_ge(exped, NT * b + t + 1)
                        dve.reciprocal(total[:, t % 2:t % 2 + 1], total[:, t % 2:t % 2 + 1]).then_inc(inverted, 1)
                        dve.wait_ge(flip_hi, NT * b + t + 1)
                        dve.tensor_tensor(pt[1][:, t % 2, 0:m, :],
                                          psum[:, 2 + t % 2, 0:m * P].rearrange("p (i c) -> p i c", c=P),
                                          pt[0][:, t % 2, 0:m, :], ALU.subtract).then_inc(flip_lo, 1)
                    dve.wait_ge(inverted, NT * (b + 1))
                    residual(b, NT - 1)



HX = 16
DX = 64
PAIRS = HX // 2
HALF = 512


def cross_attention(nc, consts, psum, x_in, x_out, dram):
    stack, sb, sem = scoped(nc)
    with stack:
        WIDE = HX * DX
        wq, wk, wv = ([sb(f"ca_w{m}{p}", [P, KC, WIDE], F16) for p in range(2)] for m in "qkv")
        wo = [sb(f"ca_wo{p}", [P, PAIRS, D], F16) for p in range(2)]
        split_weights(nc, "ca", [j for pair, matrix, cols in ((wq, dram["l1_xq"], WIDE), (wk, dram["l1_xk"], WIDE), (wv, dram["l1_xv"], WIDE),
                                                            (wo, dram["l1_xo"], D))
                                 for j in square_jobs(pair, matrix, cols)])

        n = Norm(nc, sb, sem, "ca", consts, psum, ahead=True)
        ct = [sb(f"ca_ct{p}", [P, KC, S], F16) for p in range(2)]
        qt = [[sb(f"ca_qt{a}{p}", [P, S], F16) for p in range(2)] for a in range(2)]
        kt = [[sb(f"ca_kt{a}{p}", [P, S], F16) for p in range(2)] for a in range(2)]
        v = [[sb(f"ca_v{a}{p}", [P, NT, 2 * DX], F16) for p in range(2)] for a in range(2)]
        probs = sb("ca_probs", [P, 2, S], F32)
        pt = [sb(f"ca_pt{p}", [P, 2, NT, P], F16) for p in range(2)]
        neg_max = sb("ca_neg_max", [P, 2, 2], F32)
        total = sb("ca_total", [P, 2, 2], F32)
        pair_out = sb("ca_pair_out", [P, 4, 2, DX], F32)
        ot = [sb(f"ca_ot{p}", [P, PAIRS, S], F16) for p in range(2)]
        ct_loaded = sem("ca_ct_loaded")
        projected, proj_hi, proj_lo = sem("ca_projected"), sem("ca_proj_hi"), sem("ca_proj_lo")
        scored, maxed, exped = sem("ca_scored"), sem("ca_maxed"), sem("ca_exped")
        flipped, flip_hi, flip_lo = sem("ca_flipped"), sem("ca_flip_hi"), sem("ca_flip_lo")
        weighted, inverted, normed = sem("ca_weighted"), sem("ca_inverted"), sem("ca_normed")
        o = OutProjection(ot=ot, wo=wo, bias=None, projected=sem("ca_out_projected"))
        qscale = 1.0 / (WS * DX ** 0.5)
        QK = 4
        ITEMS = QK + NT // 2
        STEPS = NT
        FLIPS = 4 * STEPS + 2
        OUT = "outputs of four steps"

        def flip_at(first, t, i):
            if i == OUT:
                return 4 * t + 1 + (t >= 4)
            return 4 * t + i - 1 + (t > 0 or i >= 2 or first) + (t > 4 or (t == 4 and i >= 2))

        def outputs_turn(t, first):
            return t == 4 or (t == 0 and not first)

        last_flip = FLIPS - 1

        def item(a, i, bank):
            if i < QK:
                out = qt[a] if i < 2 else kt[a]
                return [out[p][:, (i % 2) * HALF:(i % 2 + 1) * HALF] for p in range(2)], \
                    psum[:, bank, :], (qscale if i < 2 else 1 / WS)
            t = 2 * (i - QK)
            return [v[a][p][:, t:t + 2, :] for p in range(2)], \
                psum[:, bank, 0:4 * DX].rearrange("p (t c) -> p t c", c=2 * DX), 1 / WS

        SPARE = 7

        def first_bank(i):
            return 4 + i if i < QK else i - QK

        def flip_bank(f):
            return psum[:, 4 + f % 2, :]

        def pairs(e, body):
            body(0, 0, FIRST)
            with e.Fori(0, PAIRS // 2 - 1) as twice:
                body(twice * 2 + 1, 1, INNER)
                body(twice * 2 + 2, 0, INNER)
            body(PAIRS - 1, 1, LAST)

        FIRST, INNER, LAST = "first", "inner", "last"

        with nc.Block() as block:
            @block.sync
            def _(sp):
                def load_context(b):
                    for p in range(2):
                        sp.dma_start(ct[p][:, :, :].rearrange("p k s -> p (k s)"),
                                     dram["ctx_parts"][p][bass.ds(b * P, P), :]).then_inc(ct_loaded, 16)

                def between(b):
                    sp.wait_ge(projected, ITEMS * PAIRS * (b + 1))
                    load_context(b + 1)

                load_context(0)
                stream_ahead(sp, n, x_in, x_out, between)

            @block.gpsimd
            def _(pool):
                with pool.Fori(0, B) as b:
                    norm_gpsimd(pool, n, b)
                    norm_rows_gpsimd(pool, n, b)

            @block.tensor
            def _(pe):
                def project(b, pair, a, i, bank):
                    feats = bass.ds(pair * P, P)
                    if i < QK:
                        wt, src = (wq, n.xt) if i < 2 else (wk, ct)
                        cols = slice((i % 2) * HALF, (i % 2 + 1) * HALF)
                        for j, (k, (p, q)) in enumerate((k, term) for k in range(KC) for term in TERMS):
                            last = pe.matmul(psum[:, bank, :], wt[p][:, k, feats], src[q][:, k, cols],
                                             start=(j == 0), stop=(j == 3 * KC - 1))
                    else:
                        for s in range(2):
                            t = 2 * (i - QK) + s
                            for j, (k, (p, q)) in enumerate((k, term) for k in range(KC) for term in TERMS):
                                last = pe.matmul(psum[:, bank, s * P:(s + 1) * P], ct[p][:, k, t * P:(t + 1) * P],
                                                 wv[q][:, k, feats], start=(j == 0), stop=(j == 3 * KC - 1))
                    last.then_inc(projected, 1)

                def score(a, t):
                    for half in range(2):
                        for i, (p, q) in enumerate(TERMS):
                            for h in range(2):
                                r = slice(DX * h, DX * (h + 1))
                                last = pe.matmul(psum[:, 2 * h + half, :], qt[a][p][r, t * P:(t + 1) * P],
                                                 kt[a][q][r, half * HALF:(half + 1) * HALF],
                                                 start=(i == 0), stop=(i == 2))
                    last.then_inc(scored, 1)

                def turn(f, sources):
                    for c in range(4):
                        last = pe.transpose(flip_bank(f)[:, c * P:(c + 1) * P], sources[c], consts.ident[:, :])
                    last.then_inc(flipped, 1)

                outputs = [pair_out[:, c, :, :].rearrange("p h d -> p (h d)") for c in range(4)]

                def body(b, pair, a, place, ahead):
                    first, follows = place == FIRST, place != LAST
                    steps = STEPS * PAIRS * b + pair * STEPS
                    flips = FLIPS * PAIRS * b + pair * FLIPS
                    items = ITEMS * PAIRS * b + pair * ITEMS

                    def flip(t, i):
                        f = flip_at(first, t, i)
                        if not (first and f == 0):
                            pe.wait_ge(flip_lo, 1 + flips + f - 1)
                        h, half = i // 2, i % 2
                        pe.wait_ge(exped, 2 * steps + 2 * t + h + 1)
                        turn(f, [probs[:, h, kb * P:(kb + 1) * P] for kb in range(4 * half, 4 * half + 4)])

                    def flip_outputs(t):
                        f = flip_at(first, t, OUT)
                        pe.wait_ge(flip_lo, 1 + flips + f - 1)
                        pe.wait_ge(normed, steps + t)
                        turn(f, outputs)

                    def weigh(t, h):
                        pe.wait_ge(flip_lo, 1 + flips + flip_at(first, t, 2 * h + 1) + 1)
                        terms = [(kb, p, q) for kb in range(NT) for p, q in TERMS]
                        for j, (kb, p, q) in enumerate(terms):
                            last = pe.matmul(psum[:, 6, h * DX:(h + 1) * DX], pt[p][:, h, kb, :],
                                             v[a][q][:, kb, h * DX:(h + 1) * DX],
                                             start=(j == 0), stop=(j == len(terms) - 1))
                        if h == 1:
                            last.then_inc(weighted, 1)

                    for t in range(STEPS):
                        flip(t, 0)
                        flip(t, 1)
                        if t == 0:
                            pe.wait_ge(proj_lo, items + ITEMS)
                        if t + 1 < STEPS or follows:
                            pe.wait_ge(exped, 2 * steps + 2 * t + 2)
                        if t + 1 < STEPS:
                            score(a, t + 1)
                        elif follows:
                            pe.wait_ge(proj_lo, items + ITEMS + QK)
                            score(1 - a, 0)
                        if outputs_turn(t, first):
                            flip_outputs(t)
                        flip(t, 2)
                        if outputs_turn(t, first):
                            weigh(t, 0)
                            flip(t, 3)
                        else:
                            flip(t, 3)
                            weigh(t, 0)
                        if follows:
                            pe.wait_ge(proj_lo, items + ITEMS + t)
                            project(b, pair + 1, 1 - a, t, SPARE)
                        elif ahead:
                            pe.wait_ge(n.xn_ready, NT * (b + 1) + t + 1)
                            if t >= 1:
                                pe.wait_ge(n.xt_lo, NT * (b + 1) + t)
                            norm_flip(pe, n, b + 1, t, SPARE)
                        weigh(t, 1)

                def sequence(b, ahead):
                    pe.wait_ge(n.xt_lo, NT * (b + 1))
                    pe.wait_ge(ct_loaded, 32 * (b + 1))
                    for i in range(ITEMS):
                        if i == QK:
                            pe.wait_ge(proj_lo, ITEMS * PAIRS * b + 1)
                        project(b, 0, 0, i, first_bank(i))
                    pe.wait_ge(proj_lo, ITEMS * PAIRS * b + ITEMS)
                    score(0, 0)
                    pairs(pe, lambda pair, a, place: body(b, pair, a, place, ahead))
                    pe.wait_ge(flip_lo, 1 + FLIPS * PAIRS * (b + 1) - 1)
                    pe.wait_ge(normed, STEPS * PAIRS * (b + 1))
                    turn(last_flip, outputs)
                    pe.wait_ge(flip_lo, 1 + FLIPS * PAIRS * (b + 1))
                    out_projection_tensor(pe, n, o, b)

                norm_tensor(pe, n, 0)
                sequences(pe, sequence)

            def out_parts(pair, half):
                at = slice(pair, pair + 1) if isinstance(pair, int) else bass.ds(pair, 1)
                return [ot[p][:, at, half * HALF:(half + 1) * HALF] for p in range(2)]

            def previous_half(pair, t):
                return (pair, 0) if t == 4 else (pair - 1, 1)

            @block.scalar
            def _(act):
                def split_item(b, pair, a, i, bank):
                    out, source, scale = item(a, i, bank)
                    act.wait_ge(projected, ITEMS * PAIRS * b + pair * ITEMS + i + 1)
                    act.activation(out[0], source, ACT.Copy, scale=scale).then_inc(proj_hi, 1)

                def exponentials(steps, t):
                    for h in range(2):
                        act.wait_ge(maxed, 2 * steps + 2 * t + h + 1)
                        act.activation(probs[:, h, :], psum[:, 2 * h:2 * h + 2, :].rearrange("p a c -> p (a c)"),
                                       ACT.Exp, bias=neg_max[:, t % 2, h:h + 1],
                                       accum_out=total[:, t % 2, h:h + 1]).then_inc(exped, 1)

                def outputs_high(f, pair, half):
                    act.activation(out_parts(pair, half)[0], flip_bank(f).unsqueeze(1), ACT.Copy).then_inc(flip_hi, 1)

                def body(b, pair, a, place, ahead):
                    first, follows = place == FIRST, place != LAST
                    steps = STEPS * PAIRS * b + pair * STEPS
                    flips = FLIPS * PAIRS * b + pair * FLIPS
                    for t in range(STEPS):
                        for i in range(4):
                            f = flip_at(first, t, i)
                            h, half = i // 2, i % 2
                            act.wait_ge(flipped, flips + f + 1)
                            act.activation(pt[0][:, h, 4 * half:4 * half + 4, :],
                                           flip_bank(f).rearrange("p (c q) -> p c q", q=P),
                                           ACT.Copy).then_inc(flip_hi, 1)
                            if i == 1 and outputs_turn(t, first):
                                act.wait_ge(flipped, flips + f + 2)
                                outputs_high(f + 1, *previous_half(pair, t))
                        if t + 1 < STEPS or follows:
                            exponentials(steps, t + 1)
                        if follows:
                            split_item(b, pair + 1, 1 - a, t, SPARE)
                        elif ahead:
                            norm_high(act, n, b + 1, t, SPARE)

                def sequence(b, ahead):
                    for i in range(ITEMS):
                        split_item(b, 0, 0, i, first_bank(i))
                    exponentials(STEPS * PAIRS * b, 0)
                    pairs(act, lambda pair, a, place: body(b, pair, a, place, ahead))
                    act.wait_ge(flipped, FLIPS * PAIRS * (b + 1))
                    outputs_high(last_flip, PAIRS - 1, 1)

                norm_scalar(act, n, 0)
                sequences(act, sequence)

            @block.vector
            def _(dve):
                def split_item(b, pair, a, i, bank):
                    out, source, scale = item(a, i, bank)
                    dve.wait_ge(proj_hi, ITEMS * PAIRS * b + pair * ITEMS + i + 1)
                    dve.scalar_tensor_tensor(out=out[1], in0=source, scalar=scale, in1=out[0],
                                             op0=ALU.mult, op1=ALU.subtract).then_inc(proj_lo, 1)

                def maximum(t, h):
                    dve.tensor_reduce(out=neg_max[:, t % 2, h:h + 1],
                                      in_=psum[:, 2 * h:2 * h + 2, :].rearrange("p a c -> p (a c)"),
                                      axis=X_AXIS, op=ALU.max, negate=True).then_inc(maxed, 1)

                def outputs_low(f, pair, half):
                    hi, lo = out_parts(pair, half)
                    dve.tensor_tensor(lo, flip_bank(f).unsqueeze(1), hi, ALU.subtract).then_inc(flip_lo, 1)

                def body(b, pair, a, place, ahead):
                    first, follows = place == FIRST, place != LAST
                    steps = STEPS * PAIRS * b + pair * STEPS
                    flips = FLIPS * PAIRS * b + pair * FLIPS
                    for t in range(STEPS):
                        def low_parts(i):
                            f, h, half = flip_at(first, t, i), i // 2, i % 2
                            dve.wait_ge(flip_hi, flips + f + 1)
                            dve.tensor_tensor(pt[1][:, h, 4 * half:4 * half + 4, :],
                                              flip_bank(f).rearrange("p (c q) -> p c q", q=P),
                                              pt[0][:, h, 4 * half:4 * half + 4, :], ALU.subtract).then_inc(flip_lo, 1)

                        low_parts(0)
                        low_parts(1)
                        if outputs_turn(t, first):
                            f = flip_at(first, t, OUT)
                            dve.wait_ge(flip_hi, flips + f + 1)
                            outputs_low(f, *previous_half(pair, t))
                        scores_follow = t + 1 < STEPS or follows
                        if scores_follow:
                            dve.wait_ge(scored, steps + t + 2)
                            maximum(t + 1, 0)
                        low_parts(2)
                        low_parts(3)
                        if scores_follow:
                            maximum(t + 1, 1)
                        dve.reciprocal(total[:, t % 2, :], total[:, t % 2, :]).then_inc(inverted, 1)
                        if follows:
                            split_item(b, pair + 1, 1 - a, t, SPARE)
                        elif ahead:
                            norm_low(dve, n, b + 1, t, SPARE)
                        if first and ahead:
                            norm_stats(dve, n, b + 1, t)
                        dve.wait_ge(inverted, steps + t + 1)
                        dve.wait_ge(weighted, steps + t + 1)
                        dve.tensor_tensor(pair_out[:, t % 4, :, :],
                                          psum[:, 6, 0:2 * DX].rearrange("p (h d) -> p h d", d=DX),
                                          total[:, t % 2, :].unsqueeze(2).to_broadcast([P, 2, DX]),
                                          ALU.mult).then_inc(normed, 1)

                def sequence(b, ahead):
                    for i in range(ITEMS):
                        split_item(b, 0, 0, i, first_bank(i))
                    dve.wait_ge(scored, STEPS * PAIRS * b + 1)
                    for h in range(2):
                        maximum(0, h)

                    def pair_body(pair, a, place):
                        body(b, pair, a, place, ahead)
                        if place == FIRST and ahead:
                            norm_aggregate(dve, n, b + 1)

                    pairs(dve, pair_body)
                    dve.wait_ge(flip_hi, FLIPS * PAIRS * (b + 1))
                    outputs_low(last_flip, PAIRS - 1, 1)
                    out_projection_vector(dve, n, o, b)

                dve.memset(n.fence[:, :], 0.0).then_inc(flip_lo, 1)
                for t in range(NT):
                    norm_stats(dve, n, 0, t)
                norm_aggregate(dve, n, 0)
                for t in range(NT):
                    norm_low(dve, n, 0, t, NORM_BANKS[t % 2])
                sequences(dve, sequence)



FP8_MAX = 448.0
HALVED = 0.5
ROUNDER = 1.5 * 2.0 ** 13
FINE_BELOW = 2.0 ** -6


def fp8_ffn(nc, consts, psum, x_in, x_out, dram):
    stack, sb, sem = scoped(nc)
    with stack:
        weights = sb("ff_weights", [P, KC, D], F16)
        bias, w_scale = sb("ff_bias", [P, D], F32), sb("ff_w_scale", [P, 1], F32)
        n = Norm(nc, sb, sem, "ff", consts, psum, width=2)
        xn = sb("ff_xn_all", [P, NT, D], F32)
        amax, x_scale = sb("ff_amax", [P, NT], F32), sb("ff_x_scale", [P, NT], F32)
        half_inv, out_scale = sb("ff_half_inv", [P, NT], F32), sb("ff_out_scale", [P, NT], F32)
        coarse = sb("ff_coarse", [P, 2, D], F8)
        rounded = sb("ff_rounded", [P, 2, D], F32)
        fine = sb("ff_fine", [P, 2, D], BF16)
        is_fine = sb("ff_is_fine", [P, 2, D], U16)
        q = sb("ff_q", [P, 2, D], BF16)
        qt = sb("ff_qt", [P, KC, S], BF16)
        loaded, decoded = sem("ff_loaded"), sem("ff_decoded")
        biased, scale_step = sem("ff_biased"), sem("ff_scale_step")
        coarsened, widened, added = sem("ff_coarsened"), sem("ff_widened"), sem("ff_added")
        fined, squared, marked, merged = sem("ff_fined"), sem("ff_squared"), sem("ff_marked"), sem("ff_merged")
        flipped, flip_out, projected = sem("ff_flipped"), sem("ff_flip_out"), sem("ff_projected")
        SCALE_STEPS = NT + 3

        decode_stack, dsb, _ = scoped(nc)
        with decode_stack:
            bits8 = dsb("ff_bits8", [P, KC, D], U8)
            bits, sign = dsb("ff_bits", [P, KC, D], U16), dsb("ff_sign", [P, KC, D], U16)
            with nc.Block() as block:
                @block.sync
                def _(sp):
                    sp.dma_start(bits8[:, :, :], dram["l1_w8"].rearrange("(k p) n -> p k n", p=P)).then_inc(loaded, 16)
                    sp.dma_start(bias[:, :], dram["l1_b"].to_broadcast([P, D])).then_inc(loaded, 16)
                    sp.dma_start(w_scale[:, :], dram["l1_s"].to_broadcast([P, 1])).then_inc(loaded, 16)
                    sp.wait_ge(loaded, 48)

                @block.vector
                def _(dve):
                    dve.wait_ge(loaded, 48)
                    dve.tensor_copy(bits[:, :, :], bits8[:, :, :]).then_inc(decoded, 1)
                    dve.wait_ge(decoded, 1)
                    dve.tensor_scalar(sign[:, :, :], bits[:, :, :], 0x80, 8, ALU.bitwise_and,
                                      ALU.logical_shift_left).then_inc(decoded, 1)
                    dve.tensor_scalar(bits[:, :, :], bits[:, :, :], 0x7F, 7, ALU.bitwise_and,
                                      ALU.logical_shift_left).then_inc(decoded, 1)
                    dve.wait_ge(decoded, 3)
                    dve.tensor_tensor(bits[:, :, :], bits[:, :, :], sign[:, :, :], ALU.bitwise_or).then_inc(decoded, 1)
                    dve.wait_ge(decoded, 4)
                    dve.tensor_scalar(weights[:, :, :], bits[:, :, :].bitcast(F16), 2.0 ** 8, None,
                                      ALU.mult).then_inc(decoded, 1)
                    dve.wait_ge(decoded, 5)

        with nc.Block() as block:
            @block.sync
            def _(sp):
                stream_rows(sp, n, x_in, x_out)

            @block.gpsimd
            def _(pool):
                with pool.Fori(0, B) as b:
                    norm_gpsimd(pool, n, b)
                    for t in range(NT):
                        pool.wait_ge(n.xn_ready, NT * b + t + 1)
                        pool.tensor_tensor(n.x[:, t, :], n.x[:, t, :], bias[:, :], ALU.add).then_inc(biased, 1)

            def evacuate(act, b, t):
                act.wait_ge(flipped, NT * b + t + 1)
                act.activation(qt[:, :, t * P:(t + 1) * P],
                               psum[:, 4 + t % 2, 0:256].bitcast(BF16).rearrange("p (k c) -> p k c", c=P),
                               ACT.Copy).then_inc(flip_out, 1)

            @block.scalar
            def _(act):
                with act.Fori(0, B) as b:
                    for t in range(NT):
                        evacuate(act, b, t)

            @block.vector
            def _(dve):
                with dve.Fori(0, B) as b:
                    norm_moments(dve, n, b)
                    for t in range(NT):
                        dve.tensor_scalar(xn[:, t, :], n.x[:, t, :], n.mv[:, t, 0:1], n.rstd[:, t:t + 1],
                                          ALU.subtract, ALU.mult).then_inc(n.xn_ready, 1)
                    for t in range(NT):
                        dve.wait_ge(n.xn_ready, NT * b + t + 1)
                        dve.tensor_reduce(out=amax[:, t:t + 1], in_=xn[:, t, :], axis=X_AXIS, op=ALU.max,
                                          apply_absolute_value=True).then_inc(scale_step, 1)
                    dve.wait_ge(scale_step, SCALE_STEPS * b + NT)
                    dve.tensor_scalar(x_scale[:, :], amax[:, :], 1e-12, 1.0 / FP8_MAX, ALU.max,
                                      ALU.mult).then_inc(scale_step, 1)
                    dve.wait_ge(scale_step, SCALE_STEPS * b + NT + 1)
                    dve.tensor_scalar(out_scale[:, :], x_scale[:, :], w_scale[:, 0:1], 1 / HALVED, ALU.mult, ALU.mult)
                    dve.tensor_scalar(amax[:, :], x_scale[:, :], 1 / HALVED, None, ALU.mult).then_inc(scale_step, 1)
                    dve.wait_ge(scale_step, SCALE_STEPS * b + NT + 2)
                    dve.reciprocal(half_inv[:, :], amax[:, :]).then_inc(scale_step, 1)
                    dve.wait_ge(scale_step, SCALE_STEPS * (b + 1))
                    for t in range(NT):
                        s = t % 2
                        if t >= 2:
                            dve.wait_ge(flipped, NT * b + t - 1)
                        dve.tensor_scalar(rounded[:, s, :], xn[:, t, :], half_inv[:, t:t + 1], ROUNDER,
                                          ALU.mult, ALU.add).then_inc(added, 1)
                        dve.tensor_scalar(coarse[:, s, :], xn[:, t, :], half_inv[:, t:t + 1], None, ALU.mult,
                                          saturate=False).then_inc(coarsened, 1)
                        dve.wait_ge(added, NT * b + t + 1)
                        dve.tensor_scalar(fine[:, s, :], rounded[:, s, :], ROUNDER, None,
                                          ALU.subtract).then_inc(fined, 1)
                        dve.wait_ge(fined, NT * b + t + 1)
                        dve.tensor_tensor(rounded[:, s, :], fine[:, s, :], fine[:, s, :], ALU.mult).then_inc(squared, 1)
                        dve.wait_ge(coarsened, NT * b + t + 1)
                        dve.memset(n.fence[:, :], 0.0)
                        dve.tensor_copy(q[:, s, :], coarse[:, s, :]).then_inc(widened, 1)
                        dve.wait_ge(squared, NT * b + t + 1)
                        dve.tensor_scalar(is_fine[:, s, :], rounded[:, s, :], FINE_BELOW ** 2, None,
                                          ALU.is_lt).then_inc(marked, 1)
                        dve.wait_ge(widened, NT * b + t + 1)
                        dve.wait_ge(marked, NT * b + t + 1)
                        dve.memset(n.fence[:, :], 0.0)
                        dve.copy_predicated(q[:, s, :], is_fine[:, s, :], fine[:, s, :]).then_inc(merged, 1)
                    for t in range(NT):
                        dve.wait_ge(projected, NT * b + t + 1)
                        dve.wait_ge(biased, NT * b + t + 1)
                        dve.scalar_tensor_tensor(out=n.x[:, t, :], in0=psum[:, t % 4, :],
                                                 scalar=out_scale[:, t:t + 1], in1=n.x[:, t, :],
                                                 op0=ALU.mult, op1=ALU.add).then_inc(n.res_ready, 1)

            @block.tensor
            def _(pe):
                def project(b, t):
                    if t >= 4:
                        pe.wait_ge(n.res_ready, NT * b + t - 3)
                    pe.wait_ge(flip_out, NT * b + t + 1)
                    for k in range(KC):
                        last = pe.matmul(psum[:, t % 4, :], qt[:, k, t * P:(t + 1) * P], weights[:, k, :],
                                         start=(k == 0), stop=(k == KC - 1))
                    last.then_inc(projected, 1)

                with pe.Fori(0, B) as b:
                    for t in range(NT):
                        pe.wait_ge(merged, NT * b + t + 1)
                        if t >= 2:
                            pe.wait_ge(flip_out, NT * b + t - 1)
                        for k in range(KC):
                            last = pe.transpose(psum[:, 4 + t % 2, 0:256].bitcast(BF16)[:, k * P:(k + 1) * P],
                                                q[:, t % 2, k * P:(k + 1) * P], consts.ident_b[:, :])
                        last.then_inc(flipped, 1)
                        if t >= 1 and t < 5:
                            project(b, t - 1)
                    for t in range(4, NT):
                        project(b, t)


def program(nc, dram, subs):
    stack, sb, sem = scoped(nc)
    with stack:
        psum = stack.enter_context(nc.psum_tensor("banks", [P, 8, 512], F32))
        consts = constants(nc, sb, sem)
        dram["ctx_parts"] = [nc.dram_tensor(f"ctx_part{p}", (B * P, KC * S), F16, kind="Internal").ap()
                             for p in range(2)]
        x_in = dram["x"]
        for i, name in enumerate(subs):
            consts.turn = i
            x_out = dram["out"] if i == len(subs) - 1 else \
                nc.dram_tensor(f"x_after_{name}", (B * S, D), F32, kind="Internal").ap()
            SUB[name](nc, consts, psum, x_in, x_out, dram)
            x_in = x_out


SUB = {"window_attention": window_attention, "block_attention": block_attention, "expert_ffn": expert_ffn,
       "band_attention": band_attention, "cross_attention": cross_attention, "fp8_ffn": fp8_ffn}
ALL = tuple(SUB)


def kernel(x, ctx_1024, L0_attn_w_qkv, L0_attn_b_qkv, L0_attn_w_out, L0_attn_b_out, L0_xattn_W_out,
           L0_xattn_b_out, L0_ffn_Wg, L0_ffn_A, L0_ffn_B, L1_attn_Wq, L1_attn_bq, L1_attn_Wk, L1_attn_bk,
           L1_attn_Wv, L1_attn_bv, L1_xattn_wq, L1_xattn_wk, L1_xattn_wv, L1_xattn_wo, L1_ffn_weight,
           L1_ffn_weight_scale, L1_ffn_bias):
    import concourse.bacc as bacc
    import numpy as np
    from concourse.bass_utils import run_bass_kernel_spmd

    qkv = np.asarray(L0_attn_w_qkv).reshape(H, 3, DH, D).transpose(1, 3, 0, 2).reshape(3, D, D)
    b_qkv = np.asarray(L0_attn_b_qkv).reshape(H, 3, DH).transpose(1, 0, 2).reshape(3, 1, D)
    arrays = {
        "x": np.asarray(x).reshape(B * S, D),
        "l0_wq": qkv[0], "l0_wk": qkv[1], "l0_wv": qkv[2], "l0_wo": np.asarray(L0_attn_w_out).T,
        "l0_bq": b_qkv[0], "l0_bk": b_qkv[1], "l0_bv": b_qkv[2], "l0_bo": np.asarray(L0_attn_b_out).reshape(1, D),
        "ctx": np.asarray(ctx_1024).reshape(B * S, D),
        "ctx_t": np.asarray(ctx_1024).transpose(0, 2, 1).reshape(B * D, S),
        "l0_xo": np.asarray(L0_xattn_W_out).T, "l0_xbo": np.asarray(L0_xattn_b_out).reshape(1, D),
        "l0_g": np.asarray(L0_ffn_Wg), "l0_a": np.asarray(L0_ffn_A).transpose(1, 0, 2).reshape(D, E * R),
        "l0_b": np.asarray(L0_ffn_B).reshape(E * R, D),
        "l1_wq": np.asarray(L1_attn_Wq), "l1_wk": np.asarray(L1_attn_Wk), "l1_wv": np.asarray(L1_attn_Wv),
        "l1_bq": np.asarray(L1_attn_bq).reshape(1, D), "l1_bk": np.asarray(L1_attn_bk).reshape(1, D),
        "l1_bv": np.asarray(L1_attn_bv).reshape(1, D),
        "l1_xq": np.asarray(L1_xattn_wq).T, "l1_xk": np.asarray(L1_xattn_wk).T, "l1_xv": np.asarray(L1_xattn_wv).T,
        "l1_xo": np.asarray(L1_xattn_wo).T,
        "l1_w8": np.asarray(L1_ffn_weight).view(np.uint8).T, 
        "l1_s": np.asarray(L1_ffn_weight_scale).reshape(1, 1),
        "l1_b": np.asarray(L1_ffn_bias).reshape(1, D),
    }
    arrays = {k: np.ascontiguousarray(a) for k, a in arrays.items()}
    nc = bacc.Bacc("TRN2", target_bir_lowering=False, num_devices=1)
    dram = {k: nc.dram_tensor(f"in_{k}", a.shape, mybir.dt.from_np(a.dtype), kind="ExternalInput").ap()
            for k, a in arrays.items()}
    dram["out"] = nc.dram_tensor("out", (B * S, D), F32, kind="ExternalOutput").ap()
    program(nc, dram, ALL)
    got = run_bass_kernel_spmd(nc, [{f"in_{k}": a for k, a in arrays.items()}], core_ids=[0])
    return got.results[0]["out"].reshape(B, S, D)
```
